# Optimizing a Trainium2 kernel written in Bass

```python
import numpy as np
import jax
import jax.numpy as jnp

def _softmax(x, axis=-1):
    return jax.nn.softmax(x, axis=axis)

def _gelu(x):
    return jax.nn.gelu(x, approximate=True)

def _silu(x):
    return jax.nn.silu(x)

def _sigmoid(x):
    return jax.nn.sigmoid(x)

def _layernorm(x, axis=-1, eps=1e-05):
    m = jnp.mean(x, axis=axis, keepdims=True)
    v = jnp.var(x, axis=axis, keepdims=True)
    return (x - m) / jnp.sqrt(v + eps)

def _scatter_add(tgt, idx, src, axis=0):
    return tgt.at[idx].add(src)

def _segment_sum(src, seg, n):
    return jax.ops.segment_sum(src, seg, n)
kernel_name = 'mk_prb_d1_jaxref_r8_2d1c0c'

def setup_inputs(seed: int=0):
    np.random.seed(seed)
    _w = jnp.asarray

    def _L0_attn_setup():
        import jax, jax.numpy as jnp
        import numpy as np
        EMBED = 128
        N_HEAD = 16
        HEAD_DIM = EMBED // N_HEAD
        key = jax.random.key(seed)
        ks = jax.random.split(key, 9)

        def xavier(k, shape, fan_in, fan_out):
            bound = float(np.sqrt(6.0 / (fan_in + fan_out)))
            return jax.random.uniform(k, shape, jnp.float32, -bound, bound)
        x = jax.random.normal(ks[0], (4, 256, EMBED), jnp.float32)
        wq = xavier(ks[1], (N_HEAD, EMBED, HEAD_DIM), EMBED, HEAD_DIM)
        wk = xavier(ks[2], (N_HEAD, EMBED, HEAD_DIM), EMBED, HEAD_DIM)
        wv = xavier(ks[3], (N_HEAD, EMBED, HEAD_DIM), EMBED, HEAD_DIM)
        bq = jnp.zeros((N_HEAD, 1, HEAD_DIM), jnp.float32)
        bk = jnp.zeros((N_HEAD, 1, HEAD_DIM), jnp.float32)
        bv = jnp.zeros((N_HEAD, 1, HEAD_DIM), jnp.float32)
        bnd = 1.0 / float(np.sqrt(EMBED))
        wo = jax.random.uniform(ks[4], (EMBED, EMBED), jnp.float32, -bnd, bnd)
        bo = jax.random.uniform(ks[5], (EMBED,), jnp.float32, -bnd, bnd)
        return {'x': x, 'wq': wq, 'bq': bq, 'wk': wk, 'bk': bk, 'wv': wv, 'bv': bv, 'wo': wo, 'bo': bo}
    _L0_attn_in = _L0_attn_setup()

    def _L0_ffn_setup():
        import jax, jax.numpy as jnp
        import numpy as np
        DIM = 128

        def _reference_tuple_inner(x, W_r, W_k, W_v, mu_r, mu_k):
            B, T, C = x.shape
            x_prev = jnp.concatenate([jnp.zeros((B, 1, C), x.dtype), x[:, :-1, :]], axis=1)
            xr = mu_r * x + (1.0 - mu_r) * x_prev
            xk = mu_k * x + (1.0 - mu_k) * x_prev
            r = jax.nn.sigmoid(jnp.einsum('btc,dc->btd', xr, W_r))
            k = jnp.einsum('btc,dc->btd', xk, W_k)
            k_act = jnp.square(jax.nn.relu(k))
            out = r * jnp.einsum('btc,dc->btd', k_act, W_v)
            new_state = x[:, -1, :]
            return (out, new_state)
        key = jax.random.key(seed)
        ks = jax.random.split(key, 6)
        B, T, C = (8, 256, DIM)
        x = jax.random.normal(ks[0], (B, T, C), dtype=jnp.float32)
        s = 1.0 / np.sqrt(C)
        W_r = jax.random.uniform(ks[1], (C, C), jnp.float32, -s, s)
        W_k = jax.random.uniform(ks[2], (C, C), jnp.float32, -s, s)
        W_v = jax.random.uniform(ks[3], (C, C), jnp.float32, -s, s)
        mu_r = jax.random.uniform(ks[4], (C,), jnp.float32)
        mu_k = jax.random.uniform(ks[5], (C,), jnp.float32)
        return {'x': x, 'W_r': W_r, 'W_k': W_k, 'W_v': W_v, 'mu_r': mu_r, 'mu_k': mu_k}
    _L0_ffn_in = _L0_ffn_setup()
    _d = {'L0_attn_x': _L0_attn_in['x'], 'L0_attn_wq': _L0_attn_in['wq'], 'L0_attn_bq': _L0_attn_in['bq'], 'L0_attn_wk': _L0_attn_in['wk'], 'L0_attn_bk': _L0_attn_in['bk'], 'L0_attn_wv': _L0_attn_in['wv'], 'L0_attn_bv': _L0_attn_in['bv'], 'L0_attn_wo': _L0_attn_in['wo'], 'L0_attn_bo': _L0_attn_in['bo'], 'L0_ffn_W_r': _L0_ffn_in['W_r'], 'L0_ffn_W_k': _L0_ffn_in['W_k'], 'L0_ffn_W_v': _L0_ffn_in['W_v'], 'L0_ffn_mu_r': _L0_ffn_in['mu_r'], 'L0_ffn_mu_k': _L0_ffn_in['mu_k']}
    _x0 = _d['L0_attn_x']
    _d['L0_attn_x'] = jax.random.normal(jax.random.fold_in(jax.random.key(seed), 1), (32, 256, 128), dtype=_x0.dtype)
    del _x0
    return _d

def reference(L0_attn_x, L0_attn_wq, L0_attn_bq, L0_attn_wk, L0_attn_bk, L0_attn_wv, L0_attn_bv, L0_attn_wo, L0_attn_bo, L0_ffn_W_r, L0_ffn_W_k, L0_ffn_W_v, L0_ffn_mu_r, L0_ffn_mu_k):

    def _L0_attn_ref(x, wq, bq, wk, bk, wv, bv, wo, bo):
        import jax, jax.numpy as jnp
        import numpy as np
        EMBED = 128
        N_HEAD = 16
        HEAD_DIM = EMBED // N_HEAD
        q = jnp.einsum('bsd,hde->bhse', x, wq) + bq
        k = jnp.einsum('bsd,hde->bhse', x, wk) + bk
        v = jnp.einsum('bsd,hde->bhse', x, wv) + bv
        scale = 1.0 / jnp.sqrt(jnp.asarray(q.shape[-1], q.dtype))
        scores = jax.nn.softmax(jnp.einsum('bhse,bhte->bhst', q, k) * scale, axis=-1)
        att = jnp.einsum('bhst,bhte->bhse', scores, v)
        b, h, s, e = att.shape
        att = att.transpose(0, 2, 1, 3).reshape(b, s, h * e)
        return att @ wo.T + bo

    def _L0_ffn_ref(x, W_r, W_k, W_v, mu_r, mu_k):
        import jax, jax.numpy as jnp
        import numpy as np
        DIM = 128

        def _reference_tuple_inner(x, W_r, W_k, W_v, mu_r, mu_k):
            B, T, C = x.shape
            x_prev = jnp.concatenate([jnp.zeros((B, 1, C), x.dtype), x[:, :-1, :]], axis=1)
            xr = mu_r * x + (1.0 - mu_r) * x_prev
            xk = mu_k * x + (1.0 - mu_k) * x_prev
            r = jax.nn.sigmoid(jnp.einsum('btc,dc->btd', xr, W_r))
            k = jnp.einsum('btc,dc->btd', xk, W_k)
            k_act = jnp.square(jax.nn.relu(k))
            out = r * jnp.einsum('btc,dc->btd', k_act, W_v)
            new_state = x[:, -1, :]
            return (out, new_state)
        return _reference_tuple_inner(x, W_r, W_k, W_v, mu_r, mu_k)[0]
    x = L0_attn_x
    xn = _layernorm(x, axis=-1)
    x = x + _L0_attn_ref(xn, L0_attn_wq, L0_attn_bq, L0_attn_wk, L0_attn_bk, L0_attn_wv, L0_attn_bv, L0_attn_wo, L0_attn_bo) + _L0_ffn_ref(xn, L0_ffn_W_r, L0_ffn_W_k, L0_ffn_W_v, L0_ffn_mu_r, L0_ffn_mu_k)
    return x

_drawn_inputs = setup_inputs


def setup_inputs(seed=0):
    import zlib

    import numpy as np

    out = dict(_drawn_inputs(seed))
    spreads = {'L0_attn_bq': (0.0, 0.416), 'L0_attn_bk': (0.0, 0.8), 'L0_attn_bv': (0.0, 0.1)}
    factors = {'L0_ffn_W_r': 3.258, 'L0_ffn_mu_r': 6.394}
    for name, (base, spread) in spreads.items():
        noise = np.random.default_rng([zlib.crc32(name.encode()), seed]).standard_normal(out[name].shape)
        drawn = base * np.exp(spread * noise) if base else spread * noise
        out[name] = jnp.asarray(drawn.astype(out[name].dtype))
    for name, factor in factors.items():
        out[name] = (out[name] * factor).astype(out[name].dtype)
    return out
```

```python
from contextlib import ExitStack

import concourse.bass as bass
from concourse import mybir

F32 = mybir.dt.float32
BF16 = mybir.dt.bfloat16
ALU = mybir.AluOpType
ACT = mybir.ActivationFunctionType
AX_X = mybir.AxisListType.X

P = 128
B, S, D = 32, 256, 128
H = 16
E = D // H
ST = S // P
SCALE = float(E) ** -0.5
EPS = 1e-5
G = 4
NG = H // G
VW = 32
Q_PARTS = "hhhmlm"
K_PARTS = "mlhhhm"
TERMS = len(Q_PARTS)
KS = TERMS * E
KM = KS + 3
Q_SLOTS = {"h": (0, 3, 1), "m": (3, 6, 2), "l": (4, 5, 1)}
K_SLOTS = {"h": (2, 5, 1), "m": (0, 6, 5), "l": (1, 2, 1)}
HALF = H // 2
PR = HALF // 2

W_Q, W_K, W_V, W_O, W_R, W_KK, W_VV = range(7)
C_BQ, C_BK, C_BV, C_MUR, C_MUK = range(5)

T_FIRST, T_LAST = -3, B
LOOP = (2, 14)


def rows_of(u):
    return u // HALF, (u % HALF) // 2, u % 2


def split_attention_ffn_kernel(nc, x, weights, columns, bo, out):
    assert all(Q_PARTS[i] == p for p, s in Q_SLOTS.items() for i in range(*s))
    assert all(K_PARTS[i] == p for p, s in K_SLOTS.items() for i in range(*s))
    spill = nc.dram_tensor("spill", [2, TERMS, P, 2, S], BF16, kind="Internal").ap()

    with ExitStack() as ctx:
        def sb(name, shape, dt=F32):
            return ctx.enter_context(nc.sbuf_tensor(name, shape, dt))

        def psum(name, shape, dt=F32):
            return ctx.enter_context(nc.psum_tensor(name, shape, dt))

        def sem(name):
            return ctx.enter_context(nc.semaphore(name))

        w = sb("w", [P, 7, D])
        col = sb("col", [P, 5])
        bo_all = sb("bo_all", [P, D])
        ident = sb("ident", [P, P])
        ident16 = sb("ident16", [P, P], BF16)
        x_in = [sb(f"x_in{i}", [P, ST, D]) for i in range(2)]
        stats = sb("stats", [P, ST, 6])
        moments = sb("moments", [P, ST, 2])
        var_eps = sb("var_eps", [P, ST])
        minus_half = sb("minus_half", [P, ST])
        rstd = sb("rstd", [P, ST])
        xn = sb("xn", [P, ST, D])
        xn_t = [sb(f"xn_t{i}", [P, 1 + S]) for i in range(2)]
        qk = sb("qk", [P, 2, S])
        qk_h = sb("qk_h", [P, 2, S], BF16)
        qk_rest = sb("qk_rest", [P, 2, S])
        qk_m = sb("qk_m", [P, 2, S], BF16)
        qk_l = sb("qk_l", [P, 2, S], BF16)
        ops = [sb(f"ops{i}", [P, 2, PR, 2, S], BF16) for i in range(2)]
        neg_max = [sb(f"neg_max{i}", [P, ST, 2, PR]) for i in range(2)]
        max_rest = [sb(f"max_rest{i}", [P, ST, 2, PR]) for i in range(2)]
        zeros = sb("zeros", [P, ST, 2, PR])
        max_parts = [sb(f"max_parts{i}", [P, ST, 2, 3, PR], BF16) for i in range(2)]
        shift = [sb(f"shift{i}", [2 * 3 * PR, S], BF16) for i in range(2)]
        probs = [sb(f"probs{i}", [P, G, ST, S]) for i in range(2)]
        val = [sb(f"val{i}", [P, ST, H, VW]) for i in range(2)]
        mixed = [sb(f"mixed{i}", [P, G // 2, S]) for i in range(2)]
        inv_den = sb("inv_den", [P, 2, ST, 2 * G])
        att = sb("att", [P, ST, 2, 2 * G, E])
        att_t = sb("att_t", [P, S])
        dx = sb("dx", [P, S])
        mixed_x = sb("mixed_x", [P, 2, S])
        gate = sb("gate", [P, ST * D])
        act_r = sb("act_r", [P, S])
        act_sq = sb("act_sq", [P, S])
        ffn = sb("ffn", [P, ST * D])
        x_bo = sb("x_bo", [P, ST, D])
        rest = [sb(f"rest{i}", [P, ST * D]) for i in range(2)]
        y = [sb(f"y{i}", [P, ST * D]) for i in range(2)]

        bank_max = [psum(f"bank_max{i}", [P, ST, S]) for i in range(2)]
        bank_exp = [psum(f"bank_exp{i}", [P, ST, S]) for i in range(2)]
        bank_val = [psum(f"bank_val{i}", [P, 2, S]) for i in range(2)]
        misc = [psum(f"misc{i}", [P, 512]) for i in range(2)]

        weights_in = sem("weights_in")
        ident_zero, ident_made, consts_made = sem("ident_zero"), sem("ident_made"), sem("consts_made")
        x_in_done = [sem(f"x_in_done{i}") for i in range(2)]
        stats_done, moments_done, var_done, rstd_done = (sem("stats_done"), sem("moments_done"), sem("var_done"),
                                                         sem("rstd_done"))
        xn_done, xn_t_psum, xn_t_done = sem("xn_done"), sem("xn_t_psum"), sem("xn_t_done")
        qk_psum, qk_done = sem("qk_psum"), sem("qk_done")
        h_done, rest1_done, m_done, l_done = sem("h_done"), sem("rest1_done"), sem("m_done"), sem("l_done")
        spill_done = sem("spill_done")
        ops_in = [sem(f"ops_in{i}") for i in range(2)]
        max_scores = [sem(f"max_scores{u}") for u in range(H)]
        max_done = [sem(f"max_done{u}") for u in range(H)]
        max_h = [sem(f"max_h{i}") for i in range(2)]
        max_rest1 = [sem(f"max_rest1_{i}") for i in range(2)]
        max_m = [sem(f"max_m{i}") for i in range(2)]
        max_split = [sem(f"max_split{i}") for i in range(2)]
        shift_psum = [sem(f"shift_psum{i}") for i in range(2)]
        shift_done = [sem(f"shift_done{i}") for i in range(2)]
        shift_in = [sem(f"shift_in{i}") for i in range(2)]
        exp_scores = [sem(f"exp_scores{u}") for u in range(H)]
        exp_done = [sem(f"exp_done{u}") for u in range(H)]
        val_psum, val_done = sem("val_psum"), sem("val_done")
        mix_psum = [sem(f"mix_psum{g}") for g in range(NG)]
        mixed_done = [sem(f"mixed_done{i}") for i in range(2)]
        tokens_psum = [sem(f"tokens_psum{i}") for i in range(2)]
        inv_done = [sem(f"inv_done{i}") for i in range(2)]
        att_done = [sem(f"att_done{i}") for i in range(2)]
        att_t_psum, att_t_done, wo_psum = sem("att_t_psum"), sem("att_t_done"), sem("wo_psum")
        dx_done, mu_dx_done, mix_tokens_done = sem("dx_done"), sem("mu_dx_done"), sem("mix_tokens_done")
        gate_psum, act_r_done, gate_done = sem("gate_psum"), sem("act_r_done"), sem("gate_done")
        act_sq_done, ffn_psum, ffn_done = sem("act_sq_done"), sem("ffn_psum"), sem("ffn_done")
        x_bo_done, rest_done, y_done = sem("x_bo_done"), sem("rest_done"), sem("y_done")
        out_done = [sem(f"out_done{i}") for i in range(2)]

        N_WEIGHT_DMAS = 3

        def after(eng, semaphore, count):
            if not isinstance(count, int) or count > 0:
                eng.wait_ge(semaphore, count)

        def steps(eng, step, transfers=()):
            def straight(t):
                def n(d):
                    return min(t + d + 1, B)

                step(t, t % 2, n, lambda d, m: 16 * m * n(d), lambda d: 16 * min((t + d) // 2 + 1, B // 2),
                     lambda d: 0 <= t + d < B)

            for t in range(T_FIRST, 2 * LOOP[0]):
                straight(t)
            with eng.Fori(*LOOP) as k:
                done = {j: eng.compute_val(k * 2 + (j + 1)) for j in range(-2, 5)}
                transferred = {(j, m): eng.compute_val(k * (32 * m) + 16 * m * (j + 1))
                               for m in transfers for j in range(-1, 4)}
                pair = {j: eng.compute_val(k * 16 + 16 * (j + 1)) for j in range(-2, 3)}
                for c in range(2):
                    step(k * 2 + c, c, lambda d, c=c: done[c + d], lambda d, m, c=c: transferred[c + d, m],
                         lambda d, c=c: pair[(c + d) // 2], lambda d: True)
            for t in range(2 * LOOP[1], T_LAST + 1):
                straight(t)

        x_dram = x.rearrange("b (n p) d -> b p n d", p=P)
        out_dram = out.rearrange("b (n p) d -> b p n d", p=P)
        block = ctx.enter_context(nc.Block())

        @block.sync
        def _(sp):
            def load_x(b, parity):
                return sp.dma_start(x_in[parity][:, :, :], x_dram[b]).then_inc(x_in_done[parity], 16)

            load_x(0, 0)
            sp.dma_start(w[:, :, :], weights).then_inc(weights_in, 16)
            sp.dma_start(col[:, :], columns).then_inc(weights_in, 16)
            sp.dma_start(bo_all[:, :], bo.partition_broadcast(P)).then_inc(weights_in, 16)
            load_x(1, 1)

            def load_ops(half, p, spilled, before):
                after(sp, spill_done, spilled)
                after(sp, ops_in[half], before)
                for r in range(2):
                    src = spill[p, :, (2 * half + r) * 32:(2 * half + r + 1) * 32]
                    sp.dma_start(ops[p][64 * r:64 * r + KS, half],
                                 src.rearrange("s (e pr) a c -> s e (pr a c)", pr=PR)).then_inc(ops_in[half], 16)

            def load_shift(half, p, count, before):
                after(sp, shift_done[half], count)
                after(sp, shift_in[half], before)
                for r in range(2):
                    sp.dma_start(ops[p][64 * r + KS:64 * r + KM, half, :, 0],
                                 shift[half][r * 3 * PR:(r + 1) * 3 * PR, :]).then_inc(shift_in[half], 16)

            def step(t, p, n, moved, paired, live):
                if live(1):
                    after(sp, exp_scores[H - 1], n(-1))
                    if not live(-1):
                        sp.wait_ge(consts_made, 1)
                    load_ops(1, 1 - p, moved(1, 6), moved(0, 2))
                if live(3) and (not isinstance(t, int) or t + 3 >= 2):
                    after(sp, x_bo_done, n(1))
                    after(sp, xn_done, n(1))
                    load_x(t + 3, 1 - p)
                if live(0):
                    load_shift(1, p, n(0), moved(-1, 2))
                if live(2):
                    after(sp, ops_in[0], moved(0, 2))
                    after(sp, ops_in[1], moved(0, 2))
                    after(sp, spill_done, moved(1, 6))
                    for part, tile, made in (("h", qk_h, h_done), ("m", qk_m, m_done), ("l", qk_l, l_done)):
                        sp.wait_ge(made, n(2))
                        for a, slots in enumerate((Q_SLOTS[part], K_SLOTS[part])):
                            count = len(range(*slots))
                            dst = spill[p, slots[0]:slots[1]:slots[2], :, a].rearrange("s p c -> p s c")
                            src = tile[:, a, :].unsqueeze(1).broadcast_to([P, count, S])
                            sp.dma_start(dst, src).then_inc(spill_done, 16)
                    after(sp, exp_scores[HALF - 1], n(0))
                    if not live(0):
                        sp.wait_ge(consts_made, 1)
                    load_ops(0, p, moved(2, 6), moved(1, 2))
                if live(1):
                    load_shift(0, 1 - p, n(1), moved(0, 2))
                if live(-1):
                    sp.wait_ge(y_done, n(-1))
                    sp.dma_start(out_dram[t - 1], y[1 - p][:, :].rearrange("p (n d) -> p n d", n=ST)).then_inc(
                        out_done[1 - p], 16)

            steps(sp, step, (2, 6))
            for i in range(2):
                sp.wait_ge(out_done[i], 16 * (B // 2))

        @block.gpsimd
        def _(pool):
            nc.gpsimd.memset(ident[:, :], 0.0).then_inc(ident_zero, 1)
            pool.wait_ge(ident_zero, 1)
            nc.gpsimd.affine_select(out=ident[:, :], in_=ident[:, :], compare_op=ALU.not_equal, fill=1.0, base=0,
                                    pattern=[[-1, P]], channel_multiplier=1).then_inc(ident_made, 1)
            pool.wait_ge(weights_in, 16 * N_WEIGHT_DMAS)
            pool.wait_ge(consts_made, 1)

            def split_max(half, count, before):
                m, zero = neg_max[half], zeros[:, :, :, :]
                part = [max_parts[half][:, :, :, j, :] for j in range(3)]
                last_unit = HALF * (half + 1) - 2
                after(pool, max_done[last_unit], count)
                after(pool, shift_psum[half], before)
                nc.gpsimd.tensor_tensor(part[0], m[:, :, :, :], zero, ALU.add).then_inc(max_h[half], 1)
                pool.wait_ge(max_h[half], count)
                nc.gpsimd.tensor_tensor(max_rest[half][:, :, :, :], m[:, :, :, :], part[0],
                                        ALU.subtract).then_inc(max_rest1[half], 1)
                pool.wait_ge(max_rest1[half], count)
                nc.gpsimd.tensor_tensor(part[1], max_rest[half][:, :, :, :], zero, ALU.add).then_inc(max_m[half], 1)
                pool.wait_ge(max_m[half], count)
                nc.gpsimd.tensor_tensor(part[2], max_rest[half][:, :, :, :], part[1],
                                        ALU.subtract).then_inc(max_split[half], 1)

            def step(t, p, n, moved, paired, live):
                if live(0):
                    split_max(1, n(0), n(-1))
                if live(1):
                    pool.wait_ge(x_in_done[1 - p], paired(1))
                    after(pool, rest_done, n(0))
                    nc.gpsimd.tensor_tensor(x_bo[:, :, :], x_in[1 - p][:, :, :],
                                            bo_all[:, :].unsqueeze(1).broadcast_to([P, ST, D]),
                                            ALU.add).then_inc(x_bo_done, 1)
                    prev, cur = xn_t[1 - p][:, 0:S], xn_t[1 - p][:, 1:1 + S]
                    pool.wait_ge(xn_t_done, n(1))
                    after(pool, mix_tokens_done, n(0))
                    nc.gpsimd.tensor_tensor(dx[:, :], cur, prev, ALU.subtract).then_inc(dx_done, 1)
                    pool.wait_ge(dx_done, n(1))
                    after(pool, gate_psum, n(0))
                    nc.gpsimd.tensor_tensor(mixed_x[:, :, :], dx[:, :].unsqueeze(1).broadcast_to([P, 2, S]),
                                            col[:, C_MUR:C_MUK + 1].unsqueeze(2).broadcast_to([P, 2, S]),
                                            ALU.mult).then_inc(mu_dx_done, 1)
                    pool.wait_ge(mu_dx_done, n(1))
                    nc.gpsimd.tensor_tensor(mixed_x[:, :, :], mixed_x[:, :, :], prev.unsqueeze(1).broadcast_to([P, 2, S]),
                                            ALU.add).then_inc(mix_tokens_done, 1)
                if live(2):
                    pool.wait_ge(h_done, n(2))
                    after(pool, l_done, n(1))
                    after(pool, m_done, n(1))
                    nc.gpsimd.tensor_tensor(qk_rest[:, :, :], qk[:, :, :], qk_h[:, :, :],
                                            ALU.subtract).then_inc(rest1_done, 1)
                    pool.wait_ge(m_done, n(2))
                    after(pool, spill_done, moved(1, 6))
                    nc.gpsimd.tensor_tensor(qk_l[:, :, :], qk_rest[:, :, :], qk_m[:, :, :],
                                            ALU.subtract).then_inc(l_done, 1)
                if live(1):
                    split_max(0, n(1), n(0))
                if live(3):
                    pool.wait_ge(var_done, n(3))
                    after(pool, xn_done, n(2))
                    nc.gpsimd.tensor_tensor(rstd[:, :], var_eps[:, :], minus_half[:, :], ALU.pow).then_inc(rstd_done, 1)
                if live(1):
                    pool.wait_ge(act_r_done, n(1))
                    after(pool, ffn_psum, n(0))
                    nc.gpsimd.tensor_tensor(act_sq[:, :], act_r[:, :], act_r[:, :], ALU.mult).then_inc(act_sq_done, 1)
                    pool.wait_ge(ffn_done, n(1))
                    after(pool, y_done, n(-1))
                    pool.wait_ge(x_bo_done, n(1))
                    nc.gpsimd.tensor_tensor(rest[1 - p][:, :], ffn[:, :], x_bo[:, :, :].rearrange("p n d -> p (n d)"),
                                            ALU.add).then_inc(rest_done, 1)

            steps(pool, step, (6,))

        @block.scalar
        def _(act):
            act.wait_ge(weights_in, 16 * N_WEIGHT_DMAS)
            act.wait_ge(consts_made, 1)

            def move_mixed(i, count, before):
                act.wait_ge(mix_psum[2 * i + 1], count)
                after(act, tokens_psum[i], before)
                nc.scalar.copy(mixed[i][:, :, :], bank_val[i][:, :, :]).then_inc(mixed_done[i], 1)

            def move_shift(half, count, before):
                act.wait_ge(shift_psum[half], count)
                after(act, shift_in[half], before)
                nc.scalar.copy(shift[half][:, :], misc[1][0:2 * 3 * PR, 0:S // 2].bitcast(BF16)).then_inc(
                    shift_done[half], 1)

            def step(t, p, n, moved, paired, live):
                for u in range(H):
                    if live(0):
                        g = u // G
                        act.wait_ge(exp_scores[u], n(0))
                        if u % G == 0:
                            after(act, mix_psum[(g - 2) % NG], n(0) if g >= 2 else n(-1))
                        nc.scalar.activation(probs[g % 2][:, u % G], bank_exp[u % 2][:, :, :], ACT.Exp,
                                             scale=SCALE).then_inc(exp_done[u], 1)
                    if u == 0 and live(2):
                        act.wait_ge(xn_t_psum, n(2))
                        after(act, val_psum, n(0))
                        after(act, mix_tokens_done, n(0))
                        nc.scalar.copy(xn_t[p][:, 1:1 + S], misc[0][:, 0:S]).then_inc(xn_t_done, 1)
                    if u == 2:
                        if live(-1):
                            move_mixed(1, n(-1), n(-2))
                        if live(2):
                            act.wait_ge(qk_psum, n(2))
                            after(act, h_done, n(1))
                            after(act, rest1_done, n(1))
                            for a in range(2):
                                last = nc.scalar.activation(qk[:, a, :], misc[0][:, a * S:(a + 1) * S], ACT.Identity,
                                                            bias=col[:, C_BQ + a:C_BQ + a + 1])
                            last.then_inc(qk_done, 1)
                    if u == 3 and live(0):
                        move_shift(1, n(0), moved(-1, 2))
                    if u == 6 and live(1):
                        act.wait_ge(val_psum, n(1))
                        after(act, mix_psum[NG - 1], n(-1))
                        nc.scalar.copy(val[1 - p][:, :, :, 0:E],
                                       misc[0][:, 0:ST * D].rearrange("p (n h e) -> p n h e", n=ST, h=H)).then_inc(
                            val_done, 1)
                    if u == 7 and live(-1):
                        act.wait_ge(att_t_psum, n(-1))
                        after(act, wo_psum, n(-2))
                        nc.scalar.activation(att_t[:, :], misc[1][:, 0:S], ACT.Identity,
                                             bias=col[:, C_BV:C_BV + 1]).then_inc(att_t_done, 1)
                    if u == 9:
                        if live(0):
                            move_mixed(0, n(0), n(-1))
                        if live(1):
                            act.wait_ge(gate_psum, n(1))
                            after(act, ffn_done, n(0))
                            nc.scalar.activation(gate[:, :], misc[1][:, 0:S], ACT.Tanh,
                                                 scale=0.5).then_inc(gate_done, 1)
                            after(act, act_sq_done, n(0))
                            nc.scalar.activation(act_r[:, :], misc[1][:, S:2 * S], ACT.Relu).then_inc(act_r_done, 1)
                    if u == 11 and live(1):
                        move_shift(0, n(1), moved(0, 2))

            steps(act, step, (2,))

        @block.vector
        def _(dve):
            for i in range(2):
                nc.vector.memset(ops[i][:, :, :, :, :], 1.0)
                nc.vector.memset(val[i][:, :, :, :], 0.0)
                nc.vector.memset(xn_t[i][:, 0:1], 0.0)
            nc.vector.memset(zeros[:, :, :, :], 0.0)
            nc.vector.memset(minus_half[:, :], -0.5)
            dve.wait_ge(weights_in, 16 * N_WEIGHT_DMAS)
            nc.vector.tensor_scalar(w[:, W_VV, :], w[:, W_VV, :], 0.5, None, ALU.mult)
            dve.wait_ge(ident_made, 1)
            nc.vector.tensor_copy(ident16[:, :], ident[:, :]).then_inc(ident_zero, 1)
            dve.wait_ge(ident_zero, 2)
            for i in range(2):
                last = nc.vector.memset(val[i][:, :, :, E:E + 1], 1.0)
            last.then_inc(consts_made, 1)

            def tokens_inverse(i, count):
                dve.wait_ge(tokens_psum[i], count)
                den = misc[i][:, :].rearrange("p (n k w) -> p n k w", n=ST, w=VW)[:, :, :, E]
                nc.vector.reciprocal(inv_den[:, i], den).then_inc(inv_done[i], 1)

            def tokens_scale(i, count, before):
                dve.wait_ge(inv_done[i], count)
                after(dve, att_t_psum, before)
                num = misc[i][:, :].rearrange("p (n k w) -> p n k w", n=ST, w=VW)[:, :, :, 0:E]
                nc.vector.tensor_tensor(att[:, :, i], num,
                                        inv_den[:, i].unsqueeze(3).broadcast_to([P, ST, 2 * G, E]),
                                        ALU.mult).then_inc(att_done[i], 1)

            def step(t, p, n, moved, paired, live):
                for u in range(H):
                    if u == 8 and live(3):
                        dve.wait_ge(stats_done, n(3))
                    if live(1):
                        v = u ^ 1
                        hf, pr, r = rows_of(v)
                        dve.wait_ge(max_scores[v], n(1))
                        if u % HALF == 0:
                            after(dve, max_split[hf], n(0))
                        nc.vector.tensor_reduce(out=neg_max[hf][:, :, r, pr], in_=bank_max[v % 2][:, :, :], axis=AX_X,
                                                op=ALU.max, negate=True).then_inc(max_done[v], 1)
                    if u == 3 and live(2):
                        dve.wait_ge(qk_done, n(2))
                        after(dve, spill_done, moved(1, 6))
                        after(dve, rest1_done, n(1))
                        nc.vector.tensor_copy(qk_h[:, :, :], qk[:, :, :]).then_inc(h_done, 1)
                    if u == 5 and live(-1):
                        tokens_inverse(1, n(-1))
                    if u == 6:
                        if live(-1):
                            tokens_scale(1, n(-1), n(-2))
                        if live(2):
                            dve.wait_ge(rest1_done, n(2))
                            after(dve, l_done, n(1))
                            nc.vector.tensor_copy(qk_m[:, :, :], qk_rest[:, :, :]).then_inc(m_done, 1)
                    if u == 7 and live(3):
                        dve.wait_ge(x_in_done[1 - p], paired(3))
                        for i in range(ST):
                            last = nc.vector.bn_stats(stats[:, i, :], x_in[1 - p][:, i, :])
                        last.then_inc(stats_done, 1)
                    if u == 8 and live(3):
                        for i in range(ST):
                            last = nc.vector.bn_aggr(moments[:, i, :], stats[:, i, :])
                        last.then_inc(moments_done, 1)
                    if u == 9 and live(3):
                        dve.wait_ge(moments_done, n(3))
                        after(dve, rstd_done, n(2))
                        nc.vector.tensor_scalar(var_eps[:, :], moments[:, :, 1], EPS, None,
                                                ALU.add).then_inc(var_done, 1)
                    if u == 10 and live(3):
                        dve.wait_ge(rstd_done, n(3))
                        after(dve, xn_t_psum, n(2))
                        for i in range(ST):
                            last = nc.vector.tensor_scalar(xn[:, i, :], x_in[1 - p][:, i, :], moments[:, i, 0:1],
                                                           rstd[:, i:i + 1], ALU.subtract, ALU.mult)
                        last.then_inc(xn_done, 1)
                    if u == 11:
                        if live(-1):
                            dve.wait_ge(wo_psum, n(-1))
                            dve.wait_ge(rest_done, n(-1))
                            after(dve, out_done[1 - p], paired(-3))
                            nc.vector.tensor_tensor(y[1 - p][:, :], misc[0][:, 0:ST * D], rest[1 - p][:, :],
                                                    ALU.add).then_inc(y_done, 1)
                    if u == 13 and live(0):
                        tokens_inverse(0, n(0))
                    if u == 14 and live(0):
                        tokens_scale(0, n(0), n(-1))
                    if u == 15 and live(1):
                        dve.wait_ge(ffn_psum, n(1))
                        dve.wait_ge(gate_done, n(1))
                        after(dve, rest_done, n(0))
                        nc.vector.scalar_tensor_tensor(out=ffn[:, :], in0=gate[:, :], scalar=1.0,
                                                       in1=misc[1][:, 0:ST * D], op0=ALU.add,
                                                       op1=ALU.mult).then_inc(ffn_done, 1)

            steps(dve, step, (6,))

        @block.tensor
        def _(pe):
            pe.wait_ge(weights_in, 16 * N_WEIGHT_DMAS)
            pe.wait_ge(consts_made, 1)

            def mix_values(g, t_count, before, parity, first_val):
                pe.wait_ge(exp_done[G * g + G - 1], t_count)
                if first_val:
                    pe.wait_ge(val_done, t_count)
                if g % 2 == 0:
                    after(pe, mixed_done[g // 2], before)
                for i in range(ST):
                    for j in range(G):
                        last = nc.tensor.matmul(bank_val[g // 2][VW * j:VW * (j + 1), g % 2, :],
                                                val[parity][:, i, G * g + j, :], probs[g % 2][:, j, i, :],
                                                start=(i == 0), stop=(i == ST - 1))
                last.then_inc(mix_psum[g], 1)

            def tokens(i, count):
                pe.wait_ge(mixed_done[i], count)
                for st in range(ST):
                    for g in range(2):
                        k = st * 2 + g
                        last = nc.tensor.transpose(misc[i][:, k * P:(k + 1) * P],
                                                   mixed[i][:, g, st * P:(st + 1) * P], ident[:, :])
                last.then_inc(tokens_psum[i], 1)

            def transpose_shift(half, count):
                pe.wait_ge(max_split[half], count)
                dst = misc[1][0:2 * 3 * PR, 0:S // 2].bitcast(BF16)
                for st in range(ST):
                    last = nc.tensor.transpose(dst[:, st * P:(st + 1) * P],
                                               max_parts[half][:, st].rearrange("p r j k -> p (r j k)"),
                                               ident16[:, :])
                last.then_inc(shift_psum[half], 1)

            def step(t, p, n, moved, paired, live):
                for u in range(H):
                    v = u ^ 1
                    if live(0):
                        if u % HALF == 0:
                            pe.wait_ge(shift_in[u // HALF], moved(0, 2))
                        after(pe, exp_done[(u - 2) % H], n(0) if u >= 2 else n(-1))
                    if live(1):
                        if u % HALF == 0:
                            pe.wait_ge(ops_in[u // HALF], moved(1, 2))
                        after(pe, max_done[(v - 2) % H], n(1) if v >= 2 else n(0))
                    for i in range(ST):
                        if live(0):
                            hf, pr, r = rows_of(u)
                            q, k = (ops[p][64 * r:64 * r + KM, hf, pr, a, :] for a in range(2))
                            last = nc.tensor.matmul(bank_exp[u % 2][:, i, :], k[:, i * P:(i + 1) * P], q,
                                                    start=True, stop=True)
                            if i == ST - 1:
                                last.then_inc(exp_scores[u], 1)
                        if live(1):
                            hf, pr, r = rows_of(v)
                            q, k = (ops[1 - p][64 * r:64 * r + KS, hf, pr, a, :] for a in range(2))
                            last = nc.tensor.matmul(bank_max[v % 2][:, i, :], q[:, i * P:(i + 1) * P], k,
                                                    start=True, stop=True)
                            if i == ST - 1:
                                last.then_inc(max_scores[v], 1)
                    if u == 0 and live(2):
                        pe.wait_ge(xn_done, n(2))
                        after(pe, att_done[0], n(-1))
                        for i in range(ST):
                            last = nc.tensor.transpose(misc[0][:, i * P:(i + 1) * P], xn[:, i, :], ident[:, :])
                        last.then_inc(xn_t_psum, 1)
                    if u == 1 and live(-1):
                        mix_values(3, n(-1), n(-2), 1 - p, False)
                    if u == 2 and live(2):
                        pe.wait_ge(xn_t_done, n(2))
                        for a in range(2):
                            last = nc.tensor.matmul(misc[0][:, a * S:(a + 1) * S], w[:, W_Q + a, :],
                                                    xn_t[p][:, 1:1 + S], start=True, stop=True)
                        last.then_inc(qk_psum, 1)
                    if u == 3 and live(0):
                        pe.wait_ge(ffn_done, n(0))
                        transpose_shift(1, n(0))
                    if u == 5 and live(-1):
                        after(pe, shift_done[1], n(0))
                        tokens(1, n(-1))
                    if u == 5 and live(0):
                        mix_values(0, n(0), n(-1), p, True)
                    if u == 6 and live(1):
                        after(pe, qk_done, n(2))
                        for i in range(ST):
                            last = nc.tensor.matmul(misc[0][:, i * D:(i + 1) * D],
                                                    xn_t[1 - p][:, 1 + i * P:1 + (i + 1) * P], w[:, W_V, :],
                                                    start=True, stop=True)
                        last.then_inc(val_psum, 1)
                    if u == 7 and live(-1):
                        for i in range(2):
                            pe.wait_ge(att_done[i], n(-1))
                        for st in range(ST):
                            last = nc.tensor.transpose(misc[1][:, st * P:(st + 1) * P], att[:, st].rearrange("p i k e -> p (i k e)"),
                                                       ident[:, :])
                        last.then_inc(att_t_psum, 1)
                    if u == 9 and live(0):
                        mix_values(1, n(0), n(-1), p, False)
                    if u == 9 and live(1):
                        pe.wait_ge(mix_tokens_done, n(1))
                        after(pe, att_t_done, n(-1))
                        for i in range(ST):
                            nc.tensor.matmul(misc[1][:, i * D:(i + 1) * D], mixed_x[:, 0, i * P:(i + 1) * P], w[:, W_R, :],
                                             start=True, stop=True)
                        nc.tensor.matmul(misc[1][:, S:2 * S], w[:, W_KK, :], mixed_x[:, 1, :],
                                         start=True, stop=True).then_inc(gate_psum, 1)
                    if u == 10 and live(-1):
                        pe.wait_ge(att_t_done, n(-1))
                        after(pe, val_done, n(1))
                        for i in range(ST):
                            last = nc.tensor.matmul(misc[0][:, i * D:(i + 1) * D], att_t[:, i * P:(i + 1) * P],
                                                    w[:, W_O, :], start=True, stop=True)
                        last.then_inc(wo_psum, 1)
                    if u == 11 and live(1):
                        pe.wait_ge(gate_done, n(1))
                        pe.wait_ge(act_r_done, n(1))
                        transpose_shift(0, n(1))
                    if u == 12 and live(0):
                        after(pe, y_done, n(-1))
                        after(pe, val_done, n(1))
                        tokens(0, n(0))
                    if u == 13 and live(0):
                        mix_values(2, n(0), n(-1), p, False)
                    if u == 14 and live(1):
                        pe.wait_ge(act_sq_done, n(1))
                        pe.wait_ge(shift_done[0], n(1))
                        for i in range(ST):
                            last = nc.tensor.matmul(misc[1][:, i * D:(i + 1) * D], act_sq[:, i * P:(i + 1) * P],
                                                    w[:, W_VV, :], start=True, stop=True)
                        last.then_inc(ffn_psum, 1)

            steps(pe, step, (2,))


def kernel(L0_attn_x, L0_attn_wq, L0_attn_bq, L0_attn_wk, L0_attn_bk, L0_attn_wv, L0_attn_bv, L0_attn_wo, L0_attn_bo,
           L0_ffn_W_r, L0_ffn_W_k, L0_ffn_W_v, L0_ffn_mu_r, L0_ffn_mu_k):
    import numpy as np
    import concourse.bacc as bacc
    from concourse.bass_utils import run_bass_kernel_spmd

    def by_rows(a):
        return a.reshape(2, PR, 2, -1, E).transpose(3, 0, 2, 4, 1).reshape(-1, D)

    def by_heads(a):
        return a.transpose(1, 0, 2).reshape(-1, D)

    weights = np.stack([by_rows(np.asarray(L0_attn_wq)), by_rows(np.asarray(L0_attn_wk)),
                        by_heads(np.asarray(L0_attn_wv)), np.asarray(L0_attn_wo).T, np.asarray(L0_ffn_W_r).T,
                        np.asarray(L0_ffn_W_k).T, np.asarray(L0_ffn_W_v).T], axis=1)
    columns = np.stack([by_rows(np.asarray(L0_attn_bq))[0], by_rows(np.asarray(L0_attn_bk))[0],
                        by_heads(np.asarray(L0_attn_bv))[0], np.asarray(L0_ffn_mu_r), np.asarray(L0_ffn_mu_k)], axis=1)
    arrays = {"x": np.asarray(L0_attn_x), "weights": weights, "columns": columns, "bo": np.asarray(L0_attn_bo)}
    arrays = {name: np.ascontiguousarray(a) for name, a in arrays.items()}
    nc = bacc.Bacc("TRN2", target_bir_lowering=False, num_devices=1)
    args = [nc.dram_tensor(name, a.shape, mybir.dt.from_np(a.dtype), kind="ExternalInput").ap()
            for name, a in arrays.items()]
    args.append(nc.dram_tensor("y_out", (B, S, D), F32, kind="ExternalOutput").ap())
    split_attention_ffn_kernel(nc, *args)
    r = run_bass_kernel_spmd(nc, [arrays], core_ids=[0])
    return r.results[0]["y_out"]
```

```python
from contextlib import ExitStack

import concourse.bass as bass
from concourse import mybir

F32 = mybir.dt.float32
BF16 = mybir.dt.bfloat16
ALU = mybir.AluOpType
ACT = mybir.ActivationFunctionType
AX_X = mybir.AxisListType.X

P = 128
B, S, D = 32, 256, 128
H = 16
E = D // H
ST = S // P
SCALE = float(E) ** -0.5
EPS = 1e-5
G = 4
NG = H // G
SW = 32
VW = SW // 2
Q_PARTS = "hhhmlm"
K_PARTS = "mlhhhm"
TERMS = len(Q_PARTS)
KS = TERMS * E
RG = P // 2
KZ = P - 3
Q_SLOTS = {"h": (0, 3, 1), "m": (3, 6, 2), "l": (4, 5, 1)}
K_SLOTS = {"h": (2, 5, 1), "m": (0, 6, 5), "l": (1, 2, 1)}
HALF = H // 2
PR = HALF // 2

W_Q, W_K, W_V, W_O, W_R, W_KK, W_VV = range(7)
C_BQ, C_BK, C_BV, C_MUR, C_MUK = range(5)

T_FIRST, T_LAST = -3, B
LOOP = (2, 14)


def rows_of(u):
    return u // HALF, (u % HALF) // 2, u % 2


def split_attention_ffn_kernel(nc, x, weights, columns, bo, out):
    assert all(Q_PARTS[i] == p for p, s in Q_SLOTS.items() for i in range(*s))
    assert all(K_PARTS[i] == p for p, s in K_SLOTS.items() for i in range(*s))
    spill = nc.dram_tensor("spill", [2, 2, TERMS, P, S], BF16, kind="Internal").ap()

    with ExitStack() as ctx:
        def sb(name, shape, dt=F32):
            return ctx.enter_context(nc.sbuf_tensor(name, shape, dt))

        def psum(name, shape, dt=F32):
            return ctx.enter_context(nc.psum_tensor(name, shape, dt))

        def sem(name):
            return ctx.enter_context(nc.semaphore(name))

        w = sb("w", [P, 7, D])
        col = sb("col", [P, 5])
        bo_all = sb("bo_all", [P, D])
        ident = sb("ident", [P, P])
        ident16 = sb("ident16", [P, P], BF16)
        x_in = [sb(f"x_in{i}", [P, ST, D]) for i in range(2)]
        stats = sb("stats", [P, ST, 6])
        moments = sb("moments", [P, ST, 2])
        var_eps = sb("var_eps", [P, ST])
        minus_half = sb("minus_half", [P, ST])
        rstd = sb("rstd", [P, ST])
        xn = sb("xn", [P, ST, D])
        xn_t = [sb(f"xn_t{i}", [P, 1 + S]) for i in range(2)]
        qk = sb("qk", [P, 2, S])
        qk_h = sb("qk_h", [P, 2, S], BF16)
        qk_rest = sb("qk_rest", [P, 2, S])
        qk_m = sb("qk_m", [P, 2, S], BF16)
        qk_l = sb("qk_l", [P, 2, S], BF16)
        ops = [sb(f"ops{i}", [P, 2, 3, PR, S], BF16) for i in range(2)]
        neg_max = [sb(f"neg_max{i}", [P, ST, 2, PR]) for i in range(2)]
        max_rest = [sb(f"max_rest{i}", [P, ST, 2, PR]) for i in range(2)]
        zero_one = sb("zero_one", [P, 2])
        zeros = sb("zeros", [P, ST, 2, PR])
        max_parts = [sb(f"max_parts{i}", [P, ST, 2, 3, PR], BF16) for i in range(2)]
        shift = [sb(f"shift{i}", [2 * 3 * PR, S], BF16) for i in range(2)]
        probs = [sb(f"probs{i}", [P, G, ST, S]) for i in range(2)]
        val = [sb(f"val{i}", [P, ST, H // 2, 3, VW]) for i in range(2)]
        mixed = [sb(f"mixed{i}", [P, S]) for i in range(2)]
        inv_den = sb("inv_den", [P, 2, ST, 2 * G])
        att = sb("att", [P, ST, 2, 2 * G, E])
        att_t = sb("att_t", [P, S])
        dx = sb("dx", [P, S])
        mixed_x = [sb(f"mixed_x{i}", [P, 2, S]) for i in range(2)]
        gate = sb("gate", [P, ST * D])
        act_r = sb("act_r", [P, S])
        act_sq = sb("act_sq", [P, S])
        ffn = sb("ffn", [P, ST * D])
        x_bo = [sb(f"x_bo{i}", [P, ST, D]) for i in range(2)]
        rest = [sb(f"rest{i}", [P, ST * D]) for i in range(2)]
        y = [sb(f"y{i}", [P, ST * D]) for i in range(2)]

        bank_max = [psum(f"bank_max{i}", [P, ST, S]) for i in range(2)]
        bank_exp = [psum(f"bank_exp{i}", [P, ST, S]) for i in range(2)]
        bank_val = [psum(f"bank_val{i}", [P, 2 * S]) for i in range(2)]
        misc = [psum(f"misc{i}", [P, 512]) for i in range(2)]

        weights_in = sem("weights_in")
        ident_zero, ident_made, consts_made = sem("ident_zero"), sem("ident_made"), sem("consts_made")
        ops_made = [sem(f"ops_made{i}") for i in range(2)]
        val_made = sem("val_made")
        x_in_done = [sem(f"x_in_done{i}") for i in range(2)]
        stats_done, moments_done, var_done, rstd_done = (sem("stats_done"), sem("moments_done"), sem("var_done"),
                                                         sem("rstd_done"))
        xn_done, xn_t_psum, xn_t_done = sem("xn_done"), sem("xn_t_psum"), sem("xn_t_done")
        qk_psum = [sem(f"{a}_psum") for a in "qk"]
        qk_done = [sem(f"{a}_done") for a in "qk"]
        h_done, rest1_done, m_done, l_done = sem("h_done"), sem("rest1_done"), sem("m_done"), sem("l_done")
        spill_done = sem("spill_done")
        ops_in = [sem(f"ops_in{i}") for i in range(2)]
        max_scores = [sem(f"max_scores{u}") for u in range(H)]
        max_done = [sem(f"max_done{u}") for u in range(H)]
        max_h = [sem(f"max_h{i}") for i in range(2)]
        max_rest1 = [sem(f"max_rest1_{i}") for i in range(2)]
        max_m = [sem(f"max_m{i}") for i in range(2)]
        max_split = [sem(f"max_split{i}") for i in range(2)]
        shift_psum = [sem(f"shift_psum{i}") for i in range(2)]
        shift_done = [sem(f"shift_done{i}") for i in range(2)]
        shift_in = [sem(f"shift_in{i}") for i in range(2)]
        exp_scores = [sem(f"exp_scores{u}") for u in range(H)]
        exp_done = [sem(f"exp_done{u}") for u in range(H)]
        val_psum, val_done = sem("val_psum"), sem("val_done")
        mix_psum = [sem(f"mix_psum{g}") for g in range(NG)]
        mixed_done = [sem(f"mixed_done{i}") for i in range(2)]
        tokens_psum = [sem(f"tokens_psum{i}") for i in range(2)]
        inv_done = [sem(f"inv_done{i}") for i in range(2)]
        att_done = [sem(f"att_done{i}") for i in range(2)]
        att_t_psum, att_t_done, wo_psum = sem("att_t_psum"), sem("att_t_done"), sem("wo_psum")
        dx_done, mu_dx_done, mix_tokens_done = sem("dx_done"), sem("mu_dx_done"), sem("mix_tokens_done")
        gate_psum, act_r_done, gate_done = sem("gate_psum"), sem("act_r_done"), sem("gate_done")
        act_sq_done, ffn_psum, ffn_done = sem("act_sq_done"), sem("ffn_psum"), sem("ffn_done")
        x_bo_done, rest_done, y_done = sem("x_bo_done"), sem("rest_done"), sem("y_done")
        out_done = [sem(f"out_done{i}") for i in range(2)]

        N_WEIGHT_DMAS = 3

        def after(eng, semaphore, count):
            if not isinstance(count, int) or count > 0:
                eng.wait_ge(semaphore, count)

        def steps(eng, step, transfers=()):
            def straight(t):
                def n(d):
                    return min(t + d + 1, B)

                step(t, t % 2, n, lambda d, m: 16 * m * n(d), lambda d: 16 * min((t + d) // 2 + 1, B // 2),
                     lambda d: 0 <= t + d < B)

            for t in range(T_FIRST, 2 * LOOP[0]):
                straight(t)
            with eng.Fori(*LOOP) as k:
                done = {j: eng.compute_val(k * 2 + (j + 1)) for j in range(-2, 5)}
                transferred = {(j, m): eng.compute_val(k * (32 * m) + 16 * m * (j + 1))
                               for m in transfers for j in range(-1, 4)}
                pair = {j: eng.compute_val(k * 16 + 16 * (j + 1)) for j in range(-2, 3)}
                for c in range(2):
                    step(k * 2 + c, c, lambda d, c=c: done[c + d], lambda d, m, c=c: transferred[c + d, m],
                         lambda d, c=c: pair[(c + d) // 2], lambda d: True)
            for t in range(2 * LOOP[1], T_LAST + 1):
                straight(t)

        x_dram = x.rearrange("b (n p) d -> b p n d", p=P)
        out_dram = out.rearrange("b (n p) d -> b p n d", p=P)
        block = ctx.enter_context(nc.Block())

        @block.sync
        def _(sp):
            def load_x(b, parity):
                return sp.dma_start(x_in[parity][:, :, :], x_dram[b]).then_inc(x_in_done[parity], 16)

            load_x(0, 0)
            sp.dma_start(w[:, :, :], weights).then_inc(weights_in, 16)
            sp.dma_start(col[:, :], columns).then_inc(weights_in, 16)
            sp.dma_start(bo_all[:, :], bo.partition_broadcast(P)).then_inc(weights_in, 16)
            load_x(1, 1)

            def load_ops(half, p, spilled, before):
                after(sp, spill_done, spilled)
                after(sp, ops_in[half], before)
                for r in range(2):
                    src = spill[p].rearrange("a s (e g pr) c -> g (s e) a (pr c)", e=E, pr=PR)[2 * half + r]
                    sp.dma_start(ops[p][RG * r:RG * r + KS, half, r:3:2 - r],
                                 src).then_inc(ops_in[half], 16)

            def load_shift(half, p, count, before):
                after(sp, shift_done[half], count)
                after(sp, shift_in[half], before)
                for r in range(2):
                    sp.dma_start(ops[p][KZ:P, half, r],
                                 shift[half][r * 3 * PR:(r + 1) * 3 * PR, :]).then_inc(shift_in[half], 16)

            def spill_part(p, part, tile, made, n):
                sp.wait_ge(made, n(2))
                for a, slots in enumerate((Q_SLOTS[part], K_SLOTS[part])):
                    dst = spill[p, a, slots[0]:slots[1]:slots[2]].rearrange("s p c -> p s c")
                    src = tile[:, a, :].unsqueeze(1).broadcast_to([P, len(range(*slots)), S])
                    sp.dma_start(dst, src).then_inc(spill_done, 16)

            def step(t, p, n, moved, paired, live):
                if live(1):
                    after(sp, exp_scores[H - 1], n(-1))
                    load_ops(1, 1 - p, moved(1, 6), moved(0, 2))
                if live(0):
                    load_shift(1, p, n(0), moved(-1, 2))
                if live(2):
                    after(sp, ops_in[0], moved(0, 2))
                    after(sp, ops_in[1], moved(0, 2))
                    after(sp, spill_done, moved(1, 6))
                    spill_part(p, "h", qk_h, h_done, n)
                    spill_part(p, "m", qk_m, m_done, n)
                    spill_part(p, "l", qk_l, l_done, n)
                if live(4) and (not isinstance(t, int) or t + 4 >= 2):
                    after(sp, x_bo_done, n(2))
                    after(sp, xn_done, n(2))
                    load_x(t + 4, p)
                if live(1):
                    load_shift(0, 1 - p, n(1), moved(0, 2))
                if live(2):
                    after(sp, exp_scores[HALF - 1], n(0))
                    if not live(0):
                        sp.wait_ge(ops_made[p], 1)
                    load_ops(0, p, moved(2, 6), moved(1, 2))
                if live(-1):
                    sp.wait_ge(y_done, n(-1))
                    sp.dma_start(out_dram[t - 1], y[1 - p][:, :].rearrange("p (n d) -> p n d", n=ST)).then_inc(
                        out_done[1 - p], 16)

            steps(sp, step, (2, 6))
            for i in range(2):
                sp.wait_ge(out_done[i], 16 * (B // 2))

        @block.gpsimd
        def _(pool):
            nc.gpsimd.memset(ident[:, :], 0.0).then_inc(ident_zero, 1)
            pool.wait_ge(ident_zero, 1)
            nc.gpsimd.affine_select(out=ident[:, :], in_=ident[:, :], compare_op=ALU.not_equal, fill=1.0, base=0,
                                    pattern=[[-1, P]], channel_multiplier=1).then_inc(ident_made, 1)
            pool.wait_ge(weights_in, 16 * N_WEIGHT_DMAS)
            pool.wait_ge(consts_made, 1)

            def split_max(half, count, before):
                m, zero = neg_max[half], zeros[:, :, :, :]
                part = [max_parts[half][:, :, :, j, :] for j in range(3)]
                last_unit = HALF * (half + 1) - 2
                after(pool, max_done[last_unit], count)
                after(pool, shift_psum[half], before)
                nc.gpsimd.tensor_tensor(part[0], m[:, :, :, :], zero, ALU.add).then_inc(max_h[half], 1)
                pool.wait_ge(max_h[half], count)
                nc.gpsimd.tensor_tensor(max_rest[half][:, :, :, :], m[:, :, :, :], part[0],
                                        ALU.subtract).then_inc(max_rest1[half], 1)
                pool.wait_ge(max_rest1[half], count)
                nc.gpsimd.tensor_tensor(part[1], max_rest[half][:, :, :, :], zero, ALU.add).then_inc(max_m[half], 1)
                pool.wait_ge(max_m[half], count)
                nc.gpsimd.tensor_tensor(part[2], max_rest[half][:, :, :, :], part[1],
                                        ALU.subtract).then_inc(max_split[half], 1)

            def step(t, p, n, moved, paired, live):
                if live(0):
                    split_max(1, n(0), n(-1))
                    pool.wait_ge(ffn_done, n(0))
                    after(pool, y_done, n(-2))
                    pool.wait_ge(x_bo_done, n(0))
                    nc.gpsimd.tensor_tensor(rest[p][:, :], ffn[:, :], x_bo[p][:, :, :].rearrange("p n d -> p (n d)"),
                                            ALU.add).then_inc(rest_done, 1)
                if live(2):
                    pool.wait_ge(x_in_done[p], paired(2))
                    after(pool, rest_done, n(0))
                    nc.gpsimd.tensor_tensor(x_bo[p][:, :, :], x_in[p][:, :, :],
                                            bo_all[:, :].unsqueeze(1).broadcast_to([P, ST, D]),
                                            ALU.add).then_inc(x_bo_done, 1)
                if live(2):
                    pool.wait_ge(h_done, n(2))
                    after(pool, l_done, n(1))
                    after(pool, m_done, n(1))
                    nc.gpsimd.tensor_tensor(qk_rest[:, :, :], qk[:, :, :], qk_h[:, :, :],
                                            ALU.subtract).then_inc(rest1_done, 1)
                if live(2):
                    pool.wait_ge(m_done, n(2))
                    after(pool, spill_done, moved(1, 6))
                    nc.gpsimd.tensor_tensor(qk_l[:, :, :], qk_rest[:, :, :], qk_m[:, :, :],
                                            ALU.subtract).then_inc(l_done, 1)
                if live(3):
                    pool.wait_ge(var_done, n(3))
                    after(pool, xn_done, n(2))
                    nc.gpsimd.tensor_tensor(rstd[:, :], var_eps[:, :], minus_half[:, :], ALU.pow).then_inc(rstd_done, 1)
                if live(1):
                    split_max(0, n(1), n(0))
                if live(2):
                    prev, cur = xn_t[p][:, 0:S], xn_t[p][:, 1:1 + S]
                    mix = mixed_x[p]
                    pool.wait_ge(xn_t_done, n(2))
                    after(pool, mu_dx_done, n(1))
                    nc.gpsimd.tensor_tensor(dx[:, :], cur, prev, ALU.subtract).then_inc(dx_done, 1)
                    pool.wait_ge(dx_done, n(2))
                    after(pool, gate_psum, n(0))
                    nc.gpsimd.tensor_tensor(mix[:, :, :], dx[:, :].unsqueeze(1).broadcast_to([P, 2, S]),
                                            col[:, C_MUR:C_MUK + 1].unsqueeze(2).broadcast_to([P, 2, S]),
                                            ALU.mult).then_inc(mu_dx_done, 1)
                    pool.wait_ge(mu_dx_done, n(2))
                    nc.gpsimd.tensor_tensor(mix[:, :, :], mix[:, :, :], prev.unsqueeze(1).broadcast_to([P, 2, S]),
                                            ALU.add).then_inc(mix_tokens_done, 1)
                if live(1):
                    pool.wait_ge(act_r_done, n(1))
                    after(pool, ffn_psum, n(0))
                    nc.gpsimd.tensor_tensor(act_sq[:, :], act_r[:, :], act_r[:, :], ALU.mult).then_inc(act_sq_done, 1)

            steps(pool, step, (6,))

        @block.scalar
        def _(act):
            act.wait_ge(consts_made, 1)
            nc.scalar.copy(ops[1][:, :, 2, :, :].rearrange("p h k s -> p h (k s)"),
                           zero_one[:, 1:2].unsqueeze(2).broadcast_to([P, 2, PR * S]))
            nc.scalar.copy(ops[1][:, :, 0:2, :, :].rearrange("p h q k s -> p h (q k s)"),
                           zero_one[:, 0:1].unsqueeze(2).broadcast_to([P, 2, 2 * PR * S])).then_inc(ops_made[1], 1)
            act.wait_ge(weights_in, 16 * N_WEIGHT_DMAS)

            def move_mixed(i, count, before):
                act.wait_ge(mix_psum[2 * i + 1], count)
                after(act, tokens_psum[i], before)
                nc.scalar.copy(mixed[i][:, :], bank_val[i][:, 0:S]).then_inc(mixed_done[i], 1)

            def move_shift(half, count, before):
                act.wait_ge(shift_psum[half], count)
                after(act, shift_in[half], before)
                nc.scalar.copy(shift[half][:, :], misc[1 - half][0:2 * 3 * PR, 0:S // 2].bitcast(BF16)).then_inc(
                    shift_done[half], 1)

            def step(t, p, n, moved, paired, live):
                for u in range(H):
                    if live(0):
                        g = u // G
                        act.wait_ge(exp_scores[u], n(0))
                        if u % G == 0:
                            after(act, mix_psum[(g - 2) % NG], n(0) if g >= 2 else n(-1))
                        nc.scalar.activation(probs[g % 2][:, u % G], bank_exp[u % 2][:, :, :], ACT.Exp,
                                             scale=SCALE).then_inc(exp_done[u], 1)
                    if u in (1, 2) and live(2):
                        a = u - 1
                        act.wait_ge(qk_psum[a], n(2))
                        if a == 0:
                            after(act, h_done, n(1))
                            after(act, rest1_done, n(1))
                        nc.scalar.activation(qk[:, a, :], misc[a][:, 0:S], ACT.Identity,
                                             bias=col[:, C_BQ + a:C_BQ + a + 1]).then_inc(qk_done[a], 1)
                    if u == 2 and live(0):
                        move_shift(1, n(0), moved(-1, 2))
                    if u == 4 and live(-1):
                        move_mixed(1, n(-1), n(-2))
                    if u == 5 and live(1):
                        act.wait_ge(gate_psum, n(1))
                        after(act, ffn_done, n(0))
                        nc.scalar.activation(gate[:, :], misc[1][:, 0:S], ACT.Tanh, scale=0.5).then_inc(gate_done, 1)
                        after(act, act_sq_done, n(0))
                        nc.scalar.activation(act_r[:, :], misc[1][:, S:2 * S], ACT.Relu).then_inc(act_r_done, 1)
                    if u == 9 and live(1):
                        move_shift(0, n(1), moved(0, 2))
                    if u == 10 and live(1):
                        act.wait_ge(val_psum, n(1))
                        if not live(0):
                            act.wait_ge(val_made, 1)
                        after(act, mix_psum[NG - 1], n(-1))
                        nc.scalar.copy(val[1 - p][:, :, :, 0:3:2, 0:E].rearrange("p n k s e -> p (n k) s e"),
                                       misc[0][:, 0:ST * D].rearrange("p (k s e) -> p k s e", s=2, e=E)).then_inc(
                            val_done, 1)
                    if u == 12 and live(-1):
                        act.wait_ge(att_t_psum, n(-1))
                        after(act, wo_psum, n(-2))
                        nc.scalar.activation(att_t[:, :], misc[1][:, 0:S], ACT.Identity,
                                             bias=col[:, C_BV:C_BV + 1]).then_inc(att_t_done, 1)
                    if u == 12 and live(3):
                        act.wait_ge(xn_t_psum, n(3))
                        after(act, val_psum, n(1))
                        after(act, mix_tokens_done, n(1))
                        nc.scalar.copy(xn_t[1 - p][:, 1:1 + S], misc[0][:, 0:S]).then_inc(xn_t_done, 1)
                    if u == 14 and live(0):
                        move_mixed(0, n(0), n(-1))

            steps(act, step, (2,))

        @block.vector
        def _(dve):
            for i in range(2):
                nc.vector.memset(xn_t[i][:, 0:1], 0.0)
            nc.vector.memset(zeros[:, :, :, :], 0.0)
            nc.vector.memset(zero_one[:, 0:1], 0.0)
            nc.vector.memset(zero_one[:, 1:2], 1.0)
            nc.vector.memset(minus_half[:, :], -0.5).then_inc(consts_made, 1)
            nc.vector.memset(ops[0][:, :, 2, :, :], 1.0)

            def fill_constants():
                nc.vector.tensor_scalar(w[:, W_VV, :], w[:, W_VV, :], 0.5, None, ALU.mult)
                nc.vector.tensor_copy(ident16[:, :], ident[:, :]).then_inc(consts_made, 1)
                for i in range(2):
                    blocks = val[i][:, :, :, :, :].rearrange("p n k b w -> p (n k) b w")
                    nc.vector.memset(blocks[:, :, :, 0:E], 0.0)
                    nc.vector.memset(blocks[:, :, :, E + 1:VW], 0.0)
                    nc.vector.memset(blocks[:, :, 1, E:E + 1], 0.0)
                    last = nc.vector.memset(blocks[:, :, 0:3:2, E:E + 1], 1.0)
                last.then_inc(val_made, 1)

            def tokens_inverse(i, count):
                dve.wait_ge(tokens_psum[i], count)
                den = misc[i][:, 0:ST * P].rearrange("p (n k w) -> p n k w", n=ST, w=VW)[:, :, :, E]
                nc.vector.reciprocal(inv_den[:, i], den).then_inc(inv_done[i], 1)

            def tokens_scale(i, count, before):
                dve.wait_ge(inv_done[i], count)
                after(dve, att_t_psum, before)
                num = misc[i][:, 0:ST * P].rearrange("p (n k w) -> p n k w", n=ST, w=VW)[:, :, :, 0:E]
                nc.vector.tensor_tensor(att[:, :, i], num,
                                        inv_den[:, i].unsqueeze(3).broadcast_to([P, ST, 2 * G, E]),
                                        ALU.mult).then_inc(att_done[i], 1)

            def step(t, p, n, moved, paired, live):
                for u in range(H):
                    if u == 3 and live(2):
                        for a in range(2):
                            dve.wait_ge(qk_done[a], n(2))
                        after(dve, spill_done, moved(1, 6))
                        after(dve, rest1_done, n(1))
                        nc.vector.tensor_copy(qk_h[:, :, :], qk[:, :, :]).then_inc(h_done, 1)
                    if u == 5 and live(2):
                        dve.wait_ge(rest1_done, n(2))
                        after(dve, l_done, n(1))
                        nc.vector.tensor_copy(qk_m[:, :, :], qk_rest[:, :, :]).then_inc(m_done, 1)
                    if u == 11 and live(-1):
                        tokens_scale(1, n(-1), n(-2))
                    if u == 15 and live(-1):
                        dve.wait_ge(wo_psum, n(-1))
                        dve.wait_ge(rest_done, n(-1))
                        after(dve, out_done[1 - p], paired(-3))
                        nc.vector.tensor_tensor(y[1 - p][:, :], misc[0][:, 0:ST * D], rest[1 - p][:, :],
                                                ALU.add).then_inc(y_done, 1)
                    if u == 1 and live(3):
                        dve.wait_ge(stats_done, n(3))
                    if live(1):
                        v = u ^ 1
                        hf, pr, r = rows_of(v)
                        dve.wait_ge(max_scores[v], n(1))
                        if u % HALF == 0:
                            after(dve, max_split[hf], n(0))
                        nc.vector.tensor_reduce(out=neg_max[hf][:, :, r, pr], in_=bank_max[v % 2][:, :, :], axis=AX_X,
                                                op=ALU.max, negate=True).then_inc(max_done[v], 1)
                    if u == 0 and live(3):
                        dve.wait_ge(x_in_done[1 - p], paired(3))
                        for i in range(ST):
                            last = nc.vector.bn_stats(stats[:, i, :], x_in[1 - p][:, i, :])
                        last.then_inc(stats_done, 1)
                    if u == 1 and live(3):
                        for i in range(ST):
                            last = nc.vector.bn_aggr(moments[:, i, :], stats[:, i, :])
                        last.then_inc(moments_done, 1)
                    if u == 2 and live(3):
                        dve.wait_ge(moments_done, n(3))
                        after(dve, rstd_done, n(2))
                        nc.vector.tensor_scalar(var_eps[:, :], moments[:, :, 1], EPS, None,
                                                ALU.add).then_inc(var_done, 1)
                    if u == 6 and live(-1):
                        tokens_inverse(0, n(-1))
                    if u == 7 and live(-1):
                        tokens_scale(0, n(-1), n(-2))
                    if u == 9 and live(3):
                        dve.wait_ge(rstd_done, n(3))
                        after(dve, xn_t_psum, n(2))
                        for i in range(ST):
                            last = nc.vector.tensor_scalar(xn[:, i, :], x_in[1 - p][:, i, :], moments[:, i, 0:1],
                                                           rstd[:, i:i + 1], ALU.subtract, ALU.mult)
                        last.then_inc(xn_done, 1)
                    if u == 10:
                        if live(-1):
                            tokens_inverse(1, n(-1))
                        if live(3) and not live(2):
                            dve.wait_ge(weights_in, 16 * N_WEIGHT_DMAS)
                            dve.wait_ge(ident_made, 1)
                            fill_constants()
                            nc.vector.memset(ops[0][:, :, 0:2, :, :], 0.0).then_inc(ops_made[0], 1)
                    if u == 15 and live(1):
                        dve.wait_ge(ffn_psum, n(1))
                        dve.wait_ge(gate_done, n(1))
                        after(dve, rest_done, n(0))
                        nc.vector.scalar_tensor_tensor(out=ffn[:, :], in0=gate[:, :], scalar=1.0,
                                                       in1=misc[1][:, 0:ST * D], op0=ALU.add,
                                                       op1=ALU.mult).then_inc(ffn_done, 1)

            steps(dve, step, (6,))

        @block.tensor
        def _(pe):
            pe.wait_ge(ident_made, 1)

            def mix_values(g, i, t_count, before, parity):
                if i == 0:
                    pe.wait_ge(exp_done[G * g + G - 1], t_count)
                    if g == 0:
                        pe.wait_ge(val_done, t_count)
                    if g % 2 == 0:
                        after(pe, mixed_done[g // 2], before)
                first = g % 2 == 0
                for j in range(G):
                    weights = val[parity][:, i, G * (g // 2) + j].rearrange("p b w -> p (b w)")
                    last = nc.tensor.matmul(bank_val[g // 2][SW * j:SW * (j + 1), 0:S],
                                            weights[:, 0:SW] if first else weights[:, VW:VW + SW],
                                            probs[g % 2][:, j, i, :], start=(first and i == 0),
                                            stop=(not first and i == ST - 1))
                if i == ST - 1:
                    last.then_inc(mix_psum[g], 1)

            def tokens(i, count):
                pe.wait_ge(mixed_done[i], count)
                for st in range(ST):
                    last = nc.tensor.transpose(misc[i][:, st * P:(st + 1) * P], mixed[i][:, st * P:(st + 1) * P],
                                               ident[:, :])
                last.then_inc(tokens_psum[i], 1)

            def transpose_shift(half, count, live):
                pe.wait_ge(max_split[half], count)
                if not live(0):
                    pe.wait_ge(consts_made, 2)
                dst = misc[1 - half][0:2 * 3 * PR, 0:S // 2].bitcast(BF16)
                for st in range(ST):
                    last = nc.tensor.transpose(dst[:, st * P:(st + 1) * P],
                                               max_parts[half][:, st].rearrange("p r j k -> p (r j k)"),
                                               ident16[:, :])
                last.then_inc(shift_psum[half], 1)

            def step(t, p, n, moved, paired, live):
                for u in range(H):
                    v = u ^ 1
                    if live(0):
                        if u % HALF == 0:
                            pe.wait_ge(shift_in[u // HALF], moved(0, 2))
                        after(pe, exp_done[(u - 2) % H], n(0) if u >= 2 else n(-1))
                    if live(1):
                        if u % HALF == 0:
                            pe.wait_ge(ops_in[u // HALF], moved(1, 2))
                        after(pe, max_done[(v - 2) % H], n(1) if v >= 2 else n(0))
                    for i in range(ST):
                        if live(0):
                            hf, pr, r = rows_of(u)
                            q, k = (ops[p][:, hf, slot, pr, :] for slot in (r, 2))
                            last = nc.tensor.matmul(bank_exp[u % 2][:, i, :], k[:, i * P:(i + 1) * P], q,
                                                    start=True, stop=True)
                            if i == ST - 1:
                                last.then_inc(exp_scores[u], 1)
                        if live(1):
                            hf, pr, r = rows_of(v)
                            q, k = (ops[1 - p][0:KZ, hf, slot, pr, :] for slot in (r, 2))
                            last = nc.tensor.matmul(bank_max[v % 2][:, i, :], q[:, i * P:(i + 1) * P], k,
                                                    start=True, stop=True)
                            if i == ST - 1:
                                last.then_inc(max_scores[v], 1)
                    if u in (0, 1) and live(2):
                        a = u
                        if a == 0:
                            pe.wait_ge(xn_t_done, n(2))
                            after(pe, y_done, n(-2))
                            if not live(1):
                                pe.wait_ge(weights_in, 16 * N_WEIGHT_DMAS)
                        else:
                            after(pe, ffn_done, n(0))
                            if not live(0):
                                after(pe, qk_done[1], n(1))
                        nc.tensor.matmul(misc[a][:, 0:S], w[:, W_Q + a, :], xn_t[p][:, 1:1 + S], start=True,
                                         stop=True).then_inc(qk_psum[a], 1)
                    if u in (2, 3) and live(-1):
                        mix_values(3, u - 2, n(-1), n(-2), 1 - p)
                    if u == 2 and live(0):
                        after(pe, qk_done[0], n(2))
                        if not live(2):
                            after(pe, y_done, n(-2))
                        transpose_shift(1, n(0), live)
                    if u in (5, 7) and live(0):
                        mix_values(0, (5, 7).index(u), n(0), n(-1), p)
                    if u == 4 and live(1):
                        pe.wait_ge(mix_tokens_done, n(1))
                        after(pe, qk_done[1], n(2))
                        if not live(2):
                            after(pe, ffn_done, n(0))
                        for i in range(ST):
                            nc.tensor.matmul(misc[1][:, i * D:(i + 1) * D], mixed_x[1 - p][:, 0, i * P:(i + 1) * P],
                                             w[:, W_R, :], start=True, stop=True)
                        nc.tensor.matmul(misc[1][:, S:2 * S], w[:, W_KK, :], mixed_x[1 - p][:, 1, :],
                                         start=True, stop=True).then_inc(gate_psum, 1)
                    if u == 6 and live(-1):
                        pe.wait_ge(shift_done[1], n(0))
                        if not live(0):
                            after(pe, y_done, n(-2))
                        tokens(0, n(-1))
                    if u in (8, 10) and live(0):
                        mix_values(1, (8, 10).index(u), n(0), n(-1), p)
                    if u == 9 and live(1):
                        after(pe, att_done[0], n(-1))
                        if not live(-1):
                            after(pe, shift_done[1], n(0))
                            pe.wait_ge(qk_done[0], n(2))
                        for i in range(ST):
                            last = nc.tensor.matmul(misc[0][:, i * D:(i + 1) * D],
                                                    xn_t[1 - p][:, 1 + i * P:1 + (i + 1) * P], w[:, W_V, :],
                                                    start=True, stop=True)
                        last.then_inc(val_psum, 1)
                        pe.wait_ge(gate_done, n(1))
                        pe.wait_ge(act_r_done, n(1))
                        transpose_shift(0, n(1), live)
                    if u == 10 and live(-1):
                        after(pe, shift_done[0], n(1))
                        if not live(1):
                            after(pe, ffn_done, n(0))
                            after(pe, att_t_done, n(-2))
                        tokens(1, n(-1))
                    if u == 11 and live(3):
                        pe.wait_ge(xn_done, n(3))
                        after(pe, val_done, n(1))
                        if not live(1):
                            after(pe, qk_done[0], n(2))
                            after(pe, xn_t_done, n(2))
                        for i in range(ST):
                            last = nc.tensor.transpose(misc[0][:, i * P:(i + 1) * P], xn[:, i, :], ident[:, :])
                        last.then_inc(xn_t_psum, 1)
                    if u in (13, 14) and live(0):
                        mix_values(2, u - 13, n(0), n(-1), p)
                    if u == 12 and live(-1):
                        for i in range(2):
                            pe.wait_ge(att_done[i], n(-1))
                        for st in range(ST):
                            last = nc.tensor.transpose(misc[1][:, st * P:(st + 1) * P],
                                                       att[:, st].rearrange("p i k e -> p (i k e)"), ident[:, :])
                        last.then_inc(att_t_psum, 1)
                    if u == 14 and live(-1):
                        pe.wait_ge(att_t_done, n(-1))
                        after(pe, xn_t_done, n(3))
                        if not live(3):
                            pe.wait_ge(val_done, n(1))
                        for i in range(ST):
                            last = nc.tensor.matmul(misc[0][:, i * D:(i + 1) * D], att_t[:, i * P:(i + 1) * P],
                                                    w[:, W_O, :], start=True, stop=True)
                        last.then_inc(wo_psum, 1)
                    if u == 15 and live(1):
                        pe.wait_ge(act_sq_done, n(1))
                        after(pe, att_t_done, n(-1))
                        if not live(-1):
                            pe.wait_ge(shift_done[0], n(1))
                        for i in range(ST):
                            last = nc.tensor.matmul(misc[1][:, i * D:(i + 1) * D], act_sq[:, i * P:(i + 1) * P],
                                                    w[:, W_VV, :], start=True, stop=True)
                        last.then_inc(ffn_psum, 1)

            steps(pe, step, (2,))


def kernel(L0_attn_x, L0_attn_wq, L0_attn_bq, L0_attn_wk, L0_attn_bk, L0_attn_wv, L0_attn_bv, L0_attn_wo, L0_attn_bo,
           L0_ffn_W_r, L0_ffn_W_k, L0_ffn_W_v, L0_ffn_mu_r, L0_ffn_mu_k):
    import numpy as np
    import concourse.bacc as bacc
    from concourse.bass_utils import run_bass_kernel_spmd

    def by_rows(a):
        return a.reshape(2, PR, 2, -1, E).transpose(3, 4, 0, 2, 1).reshape(-1, D)

    def by_strips(a):
        return a.reshape(2, 2, G, *a.shape[1:]).transpose(0, 2, 1, *range(3, a.ndim + 2)).reshape(a.shape)

    def by_heads(a):
        return by_strips(a).transpose(1, 0, 2).reshape(-1, D)

    wo = by_strips(np.asarray(L0_attn_wo).T.reshape(H, E, D)).reshape(D, D)
    weights = np.stack([by_rows(np.asarray(L0_attn_wq)), by_rows(np.asarray(L0_attn_wk)),
                        by_heads(np.asarray(L0_attn_wv)), wo, np.asarray(L0_ffn_W_r).T,
                        np.asarray(L0_ffn_W_k).T, np.asarray(L0_ffn_W_v).T], axis=1)
    columns = np.stack([by_rows(np.asarray(L0_attn_bq))[0], by_rows(np.asarray(L0_attn_bk))[0],
                        by_heads(np.asarray(L0_attn_bv))[0], np.asarray(L0_ffn_mu_r), np.asarray(L0_ffn_mu_k)], axis=1)
    arrays = {"x": np.asarray(L0_attn_x), "weights": weights, "columns": columns, "bo": np.asarray(L0_attn_bo)}
    arrays = {name: np.ascontiguousarray(a) for name, a in arrays.items()}
    nc = bacc.Bacc("TRN2", target_bir_lowering=False, num_devices=1)
    args = [nc.dram_tensor(name, a.shape, mybir.dt.from_np(a.dtype), kind="ExternalInput").ap()
            for name, a in arrays.items()]
    args.append(nc.dram_tensor("y_out", (B, S, D), F32, kind="ExternalOutput").ap())
    split_attention_ffn_kernel(nc, *args)
    r = run_bass_kernel_spmd(nc, [arrays], core_ids=[0])
    return r.results[0]["y_out"]
```

```python
from contextlib import ExitStack

import concourse.bass as bass
from concourse import mybir

F32 = mybir.dt.float32
BF16 = mybir.dt.bfloat16
ALU = mybir.AluOpType
ACT = mybir.ActivationFunctionType
AX_X = mybir.AxisListType.X

P = 128
B, S, D = 32, 256, 128
H = 16
E = D // H
ST = S // P
SCALE = float(E) ** -0.5
EPS = 1e-5
G = 4
NG = H // G
SW = 32
VW = SW // 2
MW = VW + E + 1
Q_PARTS = "hhhmlm"
K_PARTS = "mlhhhm"
TERMS = len(Q_PARTS)
KS = TERMS * E
RG = P // 2
KZ = P - 3
Q_SLOTS = {"h": (0, 3, 1), "m": (3, 6, 2), "l": (4, 5, 1)}
K_SLOTS = {"h": (2, 5, 1), "m": (0, 6, 5), "l": (1, 2, 1)}
SPILLS = 5
HALF = H // 2
PR = HALF // 2

W_Q, W_K, W_V, W_O, W_R, W_KK, W_VV = range(7)
C_BQ, C_BK, C_BV, C_MUR, C_MUK = range(5)

T_FIRST, T_LAST = -3, B
TURN = 4
LOOP = (1, 7)


def rows_of(u):
    return u // HALF, (u % HALF) // 2, u % 2


def split_attention_ffn_kernel(nc, x, weights, columns, bo, out):
    assert all(Q_PARTS[i] == p for p, s in Q_SLOTS.items() for i in range(*s))
    assert all(K_PARTS[i] == p for p, s in K_SLOTS.items() for i in range(*s))
    spill = nc.dram_tensor("spill", [2, 2, TERMS, P, S], BF16, kind="Internal").ap()

    with ExitStack() as ctx:
        def sb(name, shape, dt=F32):
            return ctx.enter_context(nc.sbuf_tensor(name, shape, dt))

        def psum(name, shape, dt=F32):
            return ctx.enter_context(nc.psum_tensor(name, shape, dt))

        def sem(name):
            return ctx.enter_context(nc.semaphore(name))

        w = sb("w", [P, 7, D])
        col = sb("col", [P, 5])
        bo_all = sb("bo_all", [P, D])
        ident = sb("ident", [P, P])
        ident16 = sb("ident16", [P, P], BF16)
        x_in = [sb(f"x_in{i}", [P, ST, D]) for i in range(2)]
        stats = sb("stats", [P, ST, 6])
        moments = sb("moments", [P, ST, 2])
        var_eps = sb("var_eps", [P, ST])
        minus_half = sb("minus_half", [P, ST])
        rstd = sb("rstd", [P, ST])
        xn = sb("xn", [P, ST, D])
        xn_t = [sb(f"xn_t{i}", [P, 1 + S]) for i in range(2)]
        qk = sb("qk", [P, 2, S])
        qk_h = sb("qk_h", [P, 2, S], BF16)
        qk_rest = sb("qk_rest", [P, 2, S])
        qk_m = sb("qk_m", [P, 2, S], BF16)
        qk_l = sb("qk_l", [P, 2, S], BF16)
        ops = [sb(f"ops{i}", [P, 2, 3, PR, S], BF16) for i in range(2)]
        neg_max = [sb(f"neg_max{i}", [P, ST, 2, PR]) for i in range(2)]
        max_rest = [sb(f"max_rest{i}", [P, ST, 2, PR]) for i in range(2)]
        zero = sb("zero", [P, 1])
        zeros = sb("zeros", [P, ST, 2, PR])
        max_parts = [sb(f"max_parts{i}", [P, ST, 3, 2, PR], BF16) for i in range(2)]
        shift = [sb(f"shift{i}", [2 * 3 * PR, S], BF16) for i in range(2)]
        probs = [sb(f"probs{i}", [P, G, ST, S]) for i in range(2)]
        val = [sb(f"val{i}", [P, ST, H // 2, 3, VW]) for i in range(2)]
        mixed = [sb(f"mixed{i}", [P, S]) for i in range(2)]
        inv_den = sb("inv_den", [P, 2, ST, 2 * G])
        att = sb("att", [P, ST, 2, 2 * G, E])
        att_t = sb("att_t", [P, S])
        dx = sb("dx", [P, S])
        mixed_x = [sb(f"mixed_x{i}", [P, 2, S]) for i in range(2)]
        gate = sb("gate", [P, ST * D])
        act_r = sb("act_r", [P, S])
        act_sq = sb("act_sq", [P, S])
        ffn = sb("ffn", [P, ST * D])
        x_bo = [sb(f"x_bo{i}", [P, ST, D]) for i in range(2)]
        rest = [sb(f"rest{i}", [P, ST * D]) for i in range(2)]
        y = [sb(f"y{i}", [P, ST * D]) for i in range(2)]

        bank_max = [psum(f"bank_max{i}", [P, ST, S]) for i in range(2)]
        bank_exp = [psum(f"bank_exp{i}", [P, 2, S]) for i in range(2)]
        bank_val = [psum(f"bank_val{i}", [P, 2 * S]) for i in range(2)]
        misc = [psum(f"misc{i}", [P, 512]) for i in range(2)]

        weights_in = sem("weights_in")
        ident_zero, ident_made, consts_made = sem("ident_zero"), sem("ident_made"), sem("consts_made")
        q_zeroed = [sem(f"q_zeroed{i}") for i in range(2)]
        k_filled = [sem(f"k_filled{i}") for i in range(2)]
        val_made = sem("val_made")
        x_in_done = [sem(f"x_in_done{i}") for i in range(2)]
        stats_done, moments_done, var_done, rstd_done = (sem("stats_done"), sem("moments_done"), sem("var_done"),
                                                         sem("rstd_done"))
        xn_done, xn_t_psum, xn_t_done = sem("xn_done"), sem("xn_t_psum"), sem("xn_t_done")
        qk_psum = [sem(f"{a}_psum") for a in "qk"]
        qk_done = [sem(f"{a}_done") for a in "qk"]
        h_done, rest1_done, m_done, l_done = sem("h_done"), sem("rest1_done"), sem("m_done"), sem("l_done")
        spill_done = sem("spill_done")
        ops_in = [sem(f"ops_in{i}") for i in range(2)]
        max_scores = [sem(f"max_scores{u}") for u in range(H)]
        max_done = [sem(f"max_done{u}") for u in range(H)]
        max_h = [sem(f"max_h{i}") for i in range(2)]
        max_rest1 = [sem(f"max_rest1_{i}") for i in range(2)]
        max_m = [sem(f"max_m{i}") for i in range(2)]
        max_split = [sem(f"max_split{i}") for i in range(2)]
        shift_psum = [sem(f"shift_psum{i}") for i in range(2)]
        shift_done = [sem(f"shift_done{i}") for i in range(2)]
        shift_in = [sem(f"shift_in{i}") for i in range(2)]
        exp_scores = [sem(f"exp_scores{u}") for u in range(H)]
        exp_done = [sem(f"exp_done{u}") for u in range(H)]
        val_psum, val_done = sem("val_psum"), sem("val_done")
        mix_psum = [sem(f"mix_psum{g}") for g in range(NG)]
        mixed_done = [sem(f"mixed_done{i}") for i in range(2)]
        tokens_psum = [sem(f"tokens_psum{i}") for i in range(2)]
        inv_done = [sem(f"inv_done{i}") for i in range(2)]
        att_done = [sem(f"att_done{i}") for i in range(2)]
        att_t_psum, att_t_done, wo_psum = sem("att_t_psum"), sem("att_t_done"), sem("wo_psum")
        dx_done, mu_dx_done, mix_tokens_done = sem("dx_done"), sem("mu_dx_done"), sem("mix_tokens_done")
        gate_psum, act_r_done, gate_done = sem("gate_psum"), sem("act_r_done"), sem("gate_done")
        act_sq_done, ffn_psum, ffn_done = sem("act_sq_done"), sem("ffn_psum"), sem("ffn_done")
        x_bo_done, rest_done, y_done = sem("x_bo_done"), sem("rest_done"), sem("y_done")
        out_done = [sem(f"out_done{i}") for i in range(2)]

        N_WEIGHT_DMAS = 3

        def after(eng, semaphore, count):
            if not isinstance(count, int) or count > 0:
                eng.wait_ge(semaphore, count)

        def steps(eng, step, transfers=()):
            def straight(t):
                def n(d):
                    return min(t + d + 1, B)

                step(t, t % 2, n, lambda d, m: 16 * m * n(d), lambda d: 16 * min((t + d) // 2 + 1, B // 2),
                     lambda d: 0 <= t + d < B)

            for t in range(T_FIRST, TURN * LOOP[0]):
                straight(t)
            with eng.Fori(*LOOP) as k:
                done = {j: eng.compute_val(k * TURN + (j + 1)) for j in range(-2, TURN + 3)}
                transferred = {(j, m): eng.compute_val(k * (16 * m * TURN) + 16 * m * (j + 1))
                               for m in transfers for j in range(-1, TURN + 2)}
                pair = {j: eng.compute_val(k * (8 * TURN) + 16 * (j + 1)) for j in range(-2, TURN // 2 + 2)}
                for c in range(TURN):
                    step(k * TURN + c, c % 2, lambda d, c=c: done[c + d], lambda d, m, c=c: transferred[c + d, m],
                         lambda d, c=c: pair[(c + d) // 2], lambda d: True)
            for t in range(TURN * LOOP[1], T_LAST + 1):
                straight(t)

        x_dram = x.rearrange("b (n p) d -> b p n d", p=P)
        out_dram = out.rearrange("b (n p) d -> b p n d", p=P)
        block = ctx.enter_context(nc.Block())

        @block.sync
        def _(sp):
            def load_x(b, parity):
                return sp.dma_start(x_in[parity][:, :, :], x_dram[b]).then_inc(x_in_done[parity], 16)

            load_x(0, 0)
            sp.dma_start(w[:, :, :], weights).then_inc(weights_in, 16)
            sp.dma_start(col[:, :], columns).then_inc(weights_in, 16)
            sp.dma_start(bo_all[:, :], bo.partition_broadcast(P)).then_inc(weights_in, 16)
            load_x(1, 1)

            def load_ops(half, p, spilled, before):
                after(sp, spill_done, spilled)
                after(sp, ops_in[half], before)
                for r in range(2):
                    src = spill[p].rearrange("a s (e g pr) c -> g (s e) a (pr c)", e=E, pr=PR)[2 * half + r]
                    sp.dma_start(ops[p][RG * r:RG * r + KS, half, r:3:2 - r],
                                 src).then_inc(ops_in[half], 16)

            def load_shift(half, p, count, before):
                after(sp, shift_done[half], count)
                after(sp, shift_in[half], before)
                sp.dma_start(ops[p][KZ:P, half, 0:2].rearrange("j r k c -> j (r k) c"),
                             shift[half][:, :]).then_inc(shift_in[half], 16)

            def spill_l(p, n):
                slots = (Q_SLOTS["l"][0], TERMS + K_SLOTS["l"][0])
                sp.wait_ge(l_done, n(2))
                dst = spill[p].rearrange("a s p c -> (a s) p c")[slots[0]:slots[1] + 1:slots[1] - slots[0]]
                sp.dma_start(dst.rearrange("a p c -> p a c"), qk_l[:, :, :]).then_inc(spill_done, 16)

            def spill_part(p, part, tile, made, n):
                sp.wait_ge(made, n(2))
                for a, slots in enumerate((Q_SLOTS[part], K_SLOTS[part])):
                    dst = spill[p, a, slots[0]:slots[1]:slots[2]].rearrange("s p c -> p s c")
                    src = tile[:, a, :].unsqueeze(1).broadcast_to([P, len(range(*slots)), S])
                    sp.dma_start(dst, src).then_inc(spill_done, 16)

            def step(t, p, n, moved, paired, live):
                if live(1):
                    after(sp, exp_scores[H - 1], n(-1))
                    load_ops(1, 1 - p, moved(1, SPILLS), moved(0, 2))
                if live(0):
                    load_shift(1, p, n(0), moved(-1, 1))
                if live(2):
                    after(sp, ops_in[0], moved(0, 2))
                    after(sp, ops_in[1], moved(0, 2))
                    after(sp, spill_done, moved(1, SPILLS))
                    spill_part(p, "h", qk_h, h_done, n)
                    spill_part(p, "m", qk_m, m_done, n)
                    spill_l(p, n)
                if live(4) and (not isinstance(t, int) or t + 4 >= 2):
                    after(sp, x_bo_done, n(2))
                    after(sp, xn_done, n(2))
                    load_x(t + 4, p)
                if live(2):
                    after(sp, exp_scores[HALF - 1], n(0))
                    if not live(0):
                        sp.wait_ge(q_zeroed[p], 1)
                        sp.wait_ge(k_filled[p], 1)
                    load_ops(0, p, moved(2, SPILLS), moved(1, 2))
                if live(1):
                    load_shift(0, 1 - p, n(1), moved(0, 1))
                if live(-1):
                    sp.wait_ge(y_done, n(-1))
                    sp.dma_start(out_dram[t - 1], y[1 - p][:, :].rearrange("p (n d) -> p n d", n=ST)).then_inc(
                        out_done[1 - p], 16)

            steps(sp, step, (1, 2, SPILLS))
            for i in range(2):
                sp.wait_ge(out_done[i], 16 * (B // 2))

        @block.gpsimd
        def _(pool):
            nc.gpsimd.memset(ident[:, :], 0.0).then_inc(ident_zero, 1)
            pool.wait_ge(ident_zero, 1)
            nc.gpsimd.affine_select(out=ident[:, :], in_=ident[:, :], compare_op=ALU.not_equal, fill=1.0, base=0,
                                    pattern=[[-1, P]], channel_multiplier=1).then_inc(ident_made, 1)
            nc.gpsimd.memset(ops[1][:, :, 2, :, :], 1.0).then_inc(k_filled[1], 1)
            pool.wait_ge(weights_in, 16 * N_WEIGHT_DMAS)
            pool.wait_ge(consts_made, 1)

            def split_max(half, count, before):
                m, zero = neg_max[half], zeros[:, :, :, :]
                part = [max_parts[half][:, :, j, :, :] for j in range(3)]
                last_unit = HALF * (half + 1) - 1
                after(pool, max_done[last_unit], count)
                after(pool, shift_psum[half], before)
                nc.gpsimd.tensor_tensor(part[0], m[:, :, :, :], zero, ALU.add).then_inc(max_h[half], 1)
                pool.wait_ge(max_h[half], count)
                nc.gpsimd.tensor_tensor(max_rest[half][:, :, :, :], m[:, :, :, :], part[0],
                                        ALU.subtract).then_inc(max_rest1[half], 1)
                pool.wait_ge(max_rest1[half], count)
                nc.gpsimd.tensor_tensor(part[1], max_rest[half][:, :, :, :], zero, ALU.add).then_inc(max_m[half], 1)
                pool.wait_ge(max_m[half], count)
                nc.gpsimd.tensor_tensor(part[2], max_rest[half][:, :, :, :], part[1],
                                        ALU.subtract).then_inc(max_split[half], 1)

            def step(t, p, n, moved, paired, live):
                if live(0):
                    split_max(1, n(0), n(-1))
                    pool.wait_ge(ffn_done, n(0))
                    after(pool, y_done, n(-2))
                    pool.wait_ge(x_bo_done, n(0))
                    nc.gpsimd.tensor_tensor(rest[p][:, :], ffn[:, :], x_bo[p][:, :, :].rearrange("p n d -> p (n d)"),
                                            ALU.add).then_inc(rest_done, 1)
                if live(2):
                    pool.wait_ge(x_in_done[p], paired(2))
                    after(pool, rest_done, n(0))
                    nc.gpsimd.tensor_tensor(x_bo[p][:, :, :], x_in[p][:, :, :],
                                            bo_all[:, :].unsqueeze(1).broadcast_to([P, ST, D]),
                                            ALU.add).then_inc(x_bo_done, 1)
                if live(2):
                    pool.wait_ge(h_done, n(2))
                    after(pool, l_done, n(1))
                    after(pool, m_done, n(1))
                    nc.gpsimd.tensor_tensor(qk_rest[:, :, :], qk[:, :, :], qk_h[:, :, :],
                                            ALU.subtract).then_inc(rest1_done, 1)
                if live(2):
                    pool.wait_ge(m_done, n(2))
                    after(pool, spill_done, moved(1, SPILLS))
                    nc.gpsimd.tensor_tensor(qk_l[:, :, :], qk_rest[:, :, :], qk_m[:, :, :],
                                            ALU.subtract).then_inc(l_done, 1)
                if live(3):
                    pool.wait_ge(var_done, n(3))
                    after(pool, xn_done, n(2))
                    nc.gpsimd.tensor_tensor(rstd[:, :], var_eps[:, :], minus_half[:, :], ALU.pow).then_inc(rstd_done, 1)
                if live(1):
                    split_max(0, n(1), n(0))
                if live(2):
                    prev, cur = xn_t[p][:, 0:S], xn_t[p][:, 1:1 + S]
                    mix = mixed_x[p]
                    pool.wait_ge(xn_t_done, n(2))
                    after(pool, mu_dx_done, n(1))
                    nc.gpsimd.tensor_tensor(dx[:, :], cur, prev, ALU.subtract).then_inc(dx_done, 1)
                    pool.wait_ge(dx_done, n(2))
                    after(pool, gate_psum, n(0))
                    nc.gpsimd.tensor_tensor(mix[:, :, :], dx[:, :].unsqueeze(1).broadcast_to([P, 2, S]),
                                            col[:, C_MUR:C_MUK + 1].unsqueeze(2).broadcast_to([P, 2, S]),
                                            ALU.mult).then_inc(mu_dx_done, 1)
                    pool.wait_ge(mu_dx_done, n(2))
                    nc.gpsimd.tensor_tensor(mix[:, :, :], mix[:, :, :], prev.unsqueeze(1).broadcast_to([P, 2, S]),
                                            ALU.add).then_inc(mix_tokens_done, 1)
                if live(1):
                    pool.wait_ge(act_r_done, n(1))
                    after(pool, ffn_psum, n(0))
                    nc.gpsimd.tensor_tensor(act_sq[:, :], act_r[:, :], act_r[:, :], ALU.mult).then_inc(act_sq_done, 1)
                if live(3) and not live(2):
                    nc.gpsimd.memset(ops[0][:, :, 0:2, :, :], 0.0).then_inc(q_zeroed[0], 1)

            steps(pool, step, (SPILLS,))

        @block.scalar
        def _(act):
            act.wait_ge(consts_made, 1)
            nc.scalar.copy(ops[1][:, :, 0:2, :, :].rearrange("p h q k s -> p h (q k s)"),
                           zero[:, :].unsqueeze(2).broadcast_to([P, 2, 2 * PR * S])).then_inc(q_zeroed[1], 1)
            act.wait_ge(weights_in, 16 * N_WEIGHT_DMAS)

            def move_mixed(i, count, before):
                act.wait_ge(mix_psum[2 * i + 1], count)
                after(act, tokens_psum[i], before)
                nc.scalar.copy(mixed[i][:, :], bank_val[i][:, 0:S]).then_inc(mixed_done[i], 1)

            def move_shift(half, count, before):
                act.wait_ge(shift_psum[half], count)
                after(act, shift_in[half], before)
                nc.scalar.copy(shift[half][:, :], misc[1 - half][0:2 * 3 * PR, 0:S // 2].bitcast(BF16)).then_inc(
                    shift_done[half], 1)

            def step(t, p, n, moved, paired, live):
                for u in range(H):
                    if live(0):
                        g = u // G
                        act.wait_ge(exp_scores[u], n(0))
                        if u % G == 0:
                            after(act, mix_psum[(g - 2) % NG], n(0) if g >= 2 else n(-1))
                        j = u % G // 2 * 2
                        nc.scalar.activation(probs[g % 2][:, j:j + 2, u % 2], bank_exp[u % 2][:, :, :], ACT.Exp,
                                             scale=SCALE).then_inc(exp_done[u], 1)
                    if u in (1, 2) and live(2):
                        a = u - 1
                        act.wait_ge(qk_psum[a], n(2))
                        if a == 0:
                            after(act, h_done, n(1))
                            after(act, rest1_done, n(1))
                        nc.scalar.activation(qk[:, a, :], misc[a][:, 0:S], ACT.Identity,
                                             bias=col[:, C_BQ + a:C_BQ + a + 1]).then_inc(qk_done[a], 1)
                    if u == 2 and live(0):
                        move_shift(1, n(0), moved(-1, 1))
                    if u == 4 and live(-1):
                        move_mixed(1, n(-1), n(-2))
                    if u == 5 and live(1):
                        act.wait_ge(gate_psum, n(1))
                        after(act, ffn_done, n(0))
                        nc.scalar.activation(gate[:, :], misc[1][:, 0:S], ACT.Tanh, scale=0.5).then_inc(gate_done, 1)
                        after(act, act_sq_done, n(0))
                        nc.scalar.activation(act_r[:, :], misc[1][:, S:2 * S], ACT.Relu).then_inc(act_r_done, 1)
                    if u == 9 and live(1):
                        move_shift(0, n(1), moved(0, 1))
                    if u == 10 and live(1):
                        act.wait_ge(val_psum, n(1))
                        if not live(0):
                            act.wait_ge(val_made, 1)
                        after(act, mix_psum[NG - 1], n(-1))
                        nc.scalar.copy(val[1 - p][:, :, :, 0:3:2, 0:E].rearrange("p n k s e -> p (n k) s e"),
                                       misc[0][:, 0:ST * D].rearrange("p (k s e) -> p k s e", s=2, e=E)).then_inc(
                            val_done, 1)
                    if u == 12 and live(-1):
                        act.wait_ge(att_t_psum, n(-1))
                        after(act, wo_psum, n(-2))
                        nc.scalar.activation(att_t[:, :], misc[1][:, 0:S], ACT.Identity,
                                             bias=col[:, C_BV:C_BV + 1]).then_inc(att_t_done, 1)
                    if u == 12 and live(3):
                        act.wait_ge(xn_t_psum, n(3))
                        after(act, val_psum, n(1))
                        after(act, mix_tokens_done, n(1))
                        nc.scalar.copy(xn_t[1 - p][:, 1:1 + S], misc[0][:, 0:S]).then_inc(xn_t_done, 1)
                    if u == 14 and live(0):
                        move_mixed(0, n(0), n(-1))

            steps(act, step, (1,))

        @block.vector
        def _(dve):
            for i in range(2):
                nc.vector.memset(xn_t[i][:, 0:1], 0.0)
            nc.vector.memset(zeros[:, :, :, :], 0.0)
            nc.vector.memset(zero[:, :], 0.0)
            nc.vector.memset(minus_half[:, :], -0.5).then_inc(consts_made, 1)
            for i in range(2):
                nc.vector.memset(bank_val[i][:, 0:S], 0.0)
            nc.vector.memset(ops[0][:, :, 2, :, :], 1.0).then_inc(k_filled[0], 1)

            def fill_constants():
                nc.vector.tensor_scalar(w[:, W_VV, :], w[:, W_VV, :], 0.5, None, ALU.mult)
                nc.vector.tensor_copy(ident16[:, :], ident[:, :]).then_inc(consts_made, 1)
                for i in range(2):
                    blocks = val[i][:, :, :, :, :].rearrange("p n k b w -> p (n k) b w")
                    nc.vector.memset(blocks[:, :, :, 0:E], 0.0)
                    nc.vector.memset(blocks[:, :, :, E + 1:VW], 0.0)
                    nc.vector.memset(blocks[:, :, 1, E:E + 1], 0.0)
                    last = nc.vector.memset(blocks[:, :, 0:3:2, E:E + 1], 1.0)
                last.then_inc(val_made, 1)

            def tokens_inverse(i, count):
                dve.wait_ge(tokens_psum[i], count)
                den = misc[i][:, 0:ST * P].rearrange("p (n k w) -> p n k w", n=ST, w=VW)[:, :, :, E]
                nc.vector.reciprocal(inv_den[:, i], den).then_inc(inv_done[i], 1)

            def tokens_scale(i, count, before):
                dve.wait_ge(inv_done[i], count)
                after(dve, att_t_psum, before)
                num = misc[i][:, 0:ST * P].rearrange("p (n k w) -> p n k w", n=ST, w=VW)[:, :, :, 0:E]
                nc.vector.tensor_tensor(att[:, :, i], num,
                                        inv_den[:, i].unsqueeze(3).broadcast_to([P, ST, 2 * G, E]),
                                        ALU.mult).then_inc(att_done[i], 1)

            def step(t, p, n, moved, paired, live):
                for u in range(H):
                    if u == 3 and live(2):
                        for a in range(2):
                            dve.wait_ge(qk_done[a], n(2))
                        after(dve, spill_done, moved(1, SPILLS))
                        after(dve, rest1_done, n(1))
                        nc.vector.tensor_copy(qk_h[:, :, :], qk[:, :, :]).then_inc(h_done, 1)
                    if u == 5 and live(2):
                        dve.wait_ge(rest1_done, n(2))
                        after(dve, l_done, n(1))
                        nc.vector.tensor_copy(qk_m[:, :, :], qk_rest[:, :, :]).then_inc(m_done, 1)
                    if u == 11 and live(-1):
                        tokens_scale(1, n(-1), n(-2))
                    if u == 15 and live(-1):
                        dve.wait_ge(wo_psum, n(-1))
                        dve.wait_ge(rest_done, n(-1))
                        after(dve, out_done[1 - p], paired(-3))
                        nc.vector.tensor_tensor(y[1 - p][:, :], misc[0][:, 0:ST * D], rest[1 - p][:, :],
                                                ALU.add).then_inc(y_done, 1)
                    if u == 1 and live(3):
                        dve.wait_ge(stats_done, n(3))
                    if live(1):
                        hf, pr, r = rows_of(u)
                        dve.wait_ge(max_scores[u], n(1))
                        if u % HALF == 0:
                            after(dve, max_split[hf], n(0))
                        nc.vector.tensor_reduce(out=neg_max[hf][:, :, r, pr], in_=bank_max[r][:, :, :], axis=AX_X,
                                                op=ALU.max, negate=True).then_inc(max_done[u], 1)
                    if u == 0 and live(3):
                        dve.wait_ge(x_in_done[1 - p], paired(3))
                        for i in range(ST):
                            last = nc.vector.bn_stats(stats[:, i, :], x_in[1 - p][:, i, :])
                        last.then_inc(stats_done, 1)
                    if u == 1 and live(3):
                        for i in range(ST):
                            last = nc.vector.bn_aggr(moments[:, i, :], stats[:, i, :])
                        last.then_inc(moments_done, 1)
                    if u == 2 and live(3):
                        dve.wait_ge(moments_done, n(3))
                        after(dve, rstd_done, n(2))
                        nc.vector.tensor_scalar(var_eps[:, :], moments[:, :, 1], EPS, None,
                                                ALU.add).then_inc(var_done, 1)
                    if u == 6 and live(-1):
                        tokens_inverse(0, n(-1))
                    if u == 7 and live(-1):
                        tokens_scale(0, n(-1), n(-2))
                    if u == 9 and live(3):
                        dve.wait_ge(rstd_done, n(3))
                        after(dve, xn_t_psum, n(2))
                        for i in range(ST):
                            last = nc.vector.tensor_scalar(xn[:, i, :], x_in[1 - p][:, i, :], moments[:, i, 0:1],
                                                           rstd[:, i:i + 1], ALU.subtract, ALU.mult)
                        last.then_inc(xn_done, 1)
                    if u == 10:
                        if live(-1):
                            tokens_inverse(1, n(-1))
                        if live(3) and not live(2):
                            dve.wait_ge(weights_in, 16 * N_WEIGHT_DMAS)
                            dve.wait_ge(ident_made, 1)
                            fill_constants()
                    if u == 15 and live(1):
                        dve.wait_ge(ffn_psum, n(1))
                        dve.wait_ge(gate_done, n(1))
                        after(dve, rest_done, n(0))
                        nc.vector.scalar_tensor_tensor(out=ffn[:, :], in0=gate[:, :], scalar=1.0,
                                                       in1=misc[1][:, 0:ST * D], op0=ALU.add,
                                                       op1=ALU.mult).then_inc(ffn_done, 1)

            steps(dve, step, (SPILLS,))

        @block.tensor
        def _(pe):
            pe.wait_ge(ident_made, 1)

            def mix_values(g, i, t_count, before, parity):
                pe.wait_ge(exp_done[G * g + G - 2 + i], t_count)
                if i == 0:
                    if g == 0:
                        pe.wait_ge(val_done, t_count)
                    if g % 2 == 0:
                        after(pe, mixed_done[g // 2], before)
                first = g % 2 == 0
                for j in range(G):
                    weights = val[parity][:, i, G * (g // 2) + j].rearrange("p b w -> p (b w)")
                    last = nc.tensor.matmul(bank_val[g // 2][SW * j:SW * j + MW, 0:S],
                                            weights[:, 0:MW] if first else weights[:, VW:VW + MW],
                                            probs[g % 2][:, j, i, :], start=(first and i == 0),
                                            stop=(not first and i == ST - 1))
                if i == ST - 1:
                    last.then_inc(mix_psum[g], 1)

            def tokens(i, count):
                pe.wait_ge(mixed_done[i], count)
                for st in range(ST):
                    last = nc.tensor.transpose(misc[i][:, st * P:(st + 1) * P], mixed[i][:, st * P:(st + 1) * P],
                                               ident[:, :])
                last.then_inc(tokens_psum[i], 1)

            def transpose_shift(half, count, live):
                pe.wait_ge(max_split[half], count)
                if not live(0):
                    pe.wait_ge(consts_made, 2)
                dst = misc[1 - half][0:2 * 3 * PR, 0:S // 2].bitcast(BF16)
                for st in range(ST):
                    last = nc.tensor.transpose(dst[:, st * P:(st + 1) * P],
                                               max_parts[half][:, st].rearrange("p j r k -> p (j r k)"),
                                               ident16[:, :])
                last.then_inc(shift_psum[half], 1)

            def step(t, p, n, moved, paired, live):
                for u in range(H):
                    hf, pr, r = rows_of(u)
                    if live(0):
                        if u % HALF == 0:
                            pe.wait_ge(shift_in[u // HALF], moved(0, 1))
                        after(pe, exp_done[(u - 2) % H], n(0) if u >= 2 else n(-1))
                        nc.tensor.matmul(bank_exp[r][:, :, :], ops[p][:, hf, 2, pr, r * P:(r + 1) * P],
                                         ops[p][:, hf, 0:2, pr, :], start=True, stop=True).then_inc(exp_scores[u], 1)
                    if live(1):
                        if u % HALF == 0:
                            pe.wait_ge(ops_in[u // HALF], moved(1, 2))
                        after(pe, max_done[(u - 2) % H], n(1) if u >= 2 else n(0))
                        q, k = (ops[1 - p][0:KZ, hf, slot, pr, :] for slot in (r, 2))
                        for i in range(ST):
                            last = nc.tensor.matmul(bank_max[r][:, i, :], q[:, i * P:(i + 1) * P], k,
                                                    start=True, stop=True)
                        last.then_inc(max_scores[u], 1)
                    if u in (0, 1) and live(2):
                        a = u
                        if a == 0:
                            pe.wait_ge(xn_t_done, n(2))
                            after(pe, y_done, n(-2))
                            if not live(1):
                                pe.wait_ge(weights_in, 16 * N_WEIGHT_DMAS)
                        else:
                            after(pe, ffn_done, n(0))
                            if not live(0):
                                after(pe, qk_done[1], n(1))
                        nc.tensor.matmul(misc[a][:, 0:S], w[:, W_Q + a, :], xn_t[p][:, 1:1 + S], start=True,
                                         stop=True).then_inc(qk_psum[a], 1)
                    if u in (2, 3) and live(-1):
                        mix_values(3, u - 2, n(-1), n(-2), 1 - p)
                    if u == 2 and live(0):
                        after(pe, qk_done[0], n(2))
                        if not live(2):
                            after(pe, y_done, n(-2))
                        transpose_shift(1, n(0), live)
                    if u in (5, 7) and live(0):
                        mix_values(0, (5, 7).index(u), n(0), n(-1), p)
                    if u == 4 and live(1):
                        pe.wait_ge(mix_tokens_done, n(1))
                        after(pe, qk_done[1], n(2))
                        if not live(2):
                            after(pe, ffn_done, n(0))
                        for i in range(ST):
                            nc.tensor.matmul(misc[1][:, i * D:(i + 1) * D], mixed_x[1 - p][:, 0, i * P:(i + 1) * P],
                                             w[:, W_R, :], start=True, stop=True)
                        nc.tensor.matmul(misc[1][:, S:2 * S], w[:, W_KK, :], mixed_x[1 - p][:, 1, :],
                                         start=True, stop=True).then_inc(gate_psum, 1)
                    if u == 6 and live(-1):
                        pe.wait_ge(shift_done[1], n(0))
                        if not live(0):
                            after(pe, y_done, n(-2))
                        tokens(0, n(-1))
                    if u in (8, 10) and live(0):
                        mix_values(1, (8, 10).index(u), n(0), n(-1), p)
                    if u == 9 and live(1):
                        after(pe, att_done[0], n(-1))
                        if not live(-1):
                            after(pe, shift_done[1], n(0))
                            pe.wait_ge(qk_done[0], n(2))
                        for i in range(ST):
                            last = nc.tensor.matmul(misc[0][:, i * D:(i + 1) * D],
                                                    xn_t[1 - p][:, 1 + i * P:1 + (i + 1) * P], w[:, W_V, :],
                                                    start=True, stop=True)
                        last.then_inc(val_psum, 1)
                        pe.wait_ge(gate_done, n(1))
                        pe.wait_ge(act_r_done, n(1))
                        transpose_shift(0, n(1), live)
                    if u == 10 and live(-1):
                        after(pe, shift_done[0], n(1))
                        if not live(1):
                            after(pe, ffn_done, n(0))
                            after(pe, att_t_done, n(-2))
                        tokens(1, n(-1))
                    if u == 11 and live(3):
                        pe.wait_ge(xn_done, n(3))
                        after(pe, val_done, n(1))
                        if not live(1):
                            after(pe, qk_done[0], n(2))
                            after(pe, xn_t_done, n(2))
                        for i in range(ST):
                            last = nc.tensor.transpose(misc[0][:, i * P:(i + 1) * P], xn[:, i, :], ident[:, :])
                        last.then_inc(xn_t_psum, 1)
                    if u == 12 and live(-1):
                        for i in range(2):
                            pe.wait_ge(att_done[i], n(-1))
                        for st in range(ST):
                            last = nc.tensor.transpose(misc[1][:, st * P:(st + 1) * P],
                                                       att[:, st].rearrange("p i k e -> p (i k e)"), ident[:, :])
                        last.then_inc(att_t_psum, 1)
                    if u == 14 and live(-1):
                        pe.wait_ge(att_t_done, n(-1))
                        after(pe, xn_t_done, n(3))
                        if not live(3):
                            pe.wait_ge(val_done, n(1))
                        for i in range(ST):
                            last = nc.tensor.matmul(misc[0][:, i * D:(i + 1) * D], att_t[:, i * P:(i + 1) * P],
                                                    w[:, W_O, :], start=True, stop=True)
                        last.then_inc(wo_psum, 1)
                    if u in (13, 14) and live(0):
                        mix_values(2, u - 13, n(0), n(-1), p)
                    if u == 15 and live(1):
                        pe.wait_ge(act_sq_done, n(1))
                        after(pe, att_t_done, n(-1))
                        if not live(-1):
                            pe.wait_ge(shift_done[0], n(1))
                        for i in range(ST):
                            last = nc.tensor.matmul(misc[1][:, i * D:(i + 1) * D], act_sq[:, i * P:(i + 1) * P],
                                                    w[:, W_VV, :], start=True, stop=True)
                        last.then_inc(ffn_psum, 1)

            steps(pe, step, (1, 2))


def kernel(L0_attn_x, L0_attn_wq, L0_attn_bq, L0_attn_wk, L0_attn_bk, L0_attn_wv, L0_attn_bv, L0_attn_wo, L0_attn_bo,
           L0_ffn_W_r, L0_ffn_W_k, L0_ffn_W_v, L0_ffn_mu_r, L0_ffn_mu_k):
    import numpy as np
    import concourse.bacc as bacc
    from concourse.bass_utils import run_bass_kernel_spmd

    def by_rows(a):
        return a.reshape(2, PR, 2, -1, E).transpose(3, 4, 0, 2, 1).reshape(-1, D)

    def by_strips(a):
        return a.reshape(2, 2, G, *a.shape[1:]).transpose(0, 2, 1, *range(3, a.ndim + 2)).reshape(a.shape)

    def by_heads(a):
        return by_strips(a).transpose(1, 0, 2).reshape(-1, D)

    wo = by_strips(np.asarray(L0_attn_wo).T.reshape(H, E, D)).reshape(D, D)
    weights = np.stack([by_rows(np.asarray(L0_attn_wq)), by_rows(np.asarray(L0_attn_wk)),
                        by_heads(np.asarray(L0_attn_wv)), wo, np.asarray(L0_ffn_W_r).T,
                        np.asarray(L0_ffn_W_k).T, np.asarray(L0_ffn_W_v).T], axis=1)
    columns = np.stack([by_rows(np.asarray(L0_attn_bq))[0], by_rows(np.asarray(L0_attn_bk))[0],
                        by_heads(np.asarray(L0_attn_bv))[0], np.asarray(L0_ffn_mu_r), np.asarray(L0_ffn_mu_k)], axis=1)
    arrays = {"x": np.asarray(L0_attn_x), "weights": weights, "columns": columns, "bo": np.asarray(L0_attn_bo)}
    arrays = {name: np.ascontiguousarray(a) for name, a in arrays.items()}
    nc = bacc.Bacc("TRN2", target_bir_lowering=False, num_devices=1)
    args = [nc.dram_tensor(name, a.shape, mybir.dt.from_np(a.dtype), kind="ExternalInput").ap()
            for name, a in arrays.items()]
    args.append(nc.dram_tensor("y_out", (B, S, D), F32, kind="ExternalOutput").ap())
    split_attention_ffn_kernel(nc, *args)
    r = run_bass_kernel_spmd(nc, [arrays], core_ids=[0])
    return r.results[0]["y_out"]
```
